# Optimizing a Trainium2 kernel written in Bass

```python
import numpy as np
import jax
import jax.numpy as jnp

def _softmax(x, axis=-1):
    return jax.nn.softmax(x, axis=axis)
def _gelu(x):
    return jax.nn.gelu(x, approximate=True)
def _silu(x):
    return jax.nn.silu(x)
def _sigmoid(x):
    return jax.nn.sigmoid(x)
def _layernorm(x, axis=-1, eps=1e-5):
    m = jnp.mean(x, axis=axis, keepdims=True)
    v = jnp.var(x, axis=axis, keepdims=True)
    return (x - m) / jnp.sqrt(v + eps)
def _scatter_add(tgt, idx, src, axis=0):
    return tgt.at[idx].add(src)
def _segment_sum(src, seg, n):
    return jax.ops.segment_sum(src, seg, n)

kernel_name = 'mk_adj_resnorm_d4_adj_64_d46c98'

def setup_inputs(seed: int = 0):
    np.random.seed(seed)
    _w = jnp.asarray
    def _rec_inputs():
        import jax
        import jax.numpy as jnp
        _gk = jax.random.key(seed)
        x = -0.000929 + 1 * jax.random.normal(jax.random.fold_in(_gk, 1), (3327, 64), jnp.float32)
        _w = (1.0 + jnp.arange(3327, dtype=jnp.float32)) ** -0.5
        _w = _w / _w.mean()
        _pij = jnp.clip(0.00961827 * _w[:, None] * _w[None, :], 0.0, 1.0)
        _a = jax.random.uniform(jax.random.fold_in(_gk, 2), (3327, 3327)) < _pij
        _a = jnp.logical_or(_a, jnp.eye(3327, dtype=bool))
        _af = _a.astype(jnp.float32)
        _af = _af * jax.random.uniform(jax.random.fold_in(_gk, 3), (3327, 3327), jnp.float32, 0.05, 1)
        adj = _af
        return x, adj
    x, adj = _rec_inputs()
    def _L0_gnn_setup():
        import jax, jax.numpy as jnp
        import numpy as np
        N = 16384
        F_IN = 64
        F_OUT = 64
        key = jax.random.key(seed)
        k1, k2, k3 = jax.random.split(key, 3)
        features = jax.random.normal(k1, (N, F_IN), dtype=jnp.float32)
        adj = jax.random.uniform(k2, (N, N), dtype=jnp.float32)
        W = jax.random.normal(k3, (F_OUT, 2 * F_IN), dtype=jnp.float32)
        return {'features': features, 'adj': adj, 'W': W}
    _L0_gnn_all = _L0_gnn_setup()
    _L0_gnn_in = {k: v for k, v in _L0_gnn_all.items() if k in ('W', )}
    del _L0_gnn_all

    def _L1_gnn_setup():
        import jax, jax.numpy as jnp
        import numpy as np
        CURV = 1.0
        MIN_NORM = 1e-15
        TANH_CLIP = 1.0 - 1e-05

        def _mobius_add(x, y, c):
            x2 = jnp.sum(x * x, axis=-1, keepdims=True)
            y2 = jnp.sum(y * y, axis=-1, keepdims=True)
            xy = jnp.sum(x * y, axis=-1, keepdims=True)
            num = (1.0 + 2.0 * c * xy + c * y2) * x + (1.0 - c * x2) * y
            den = 1.0 + 2.0 * c * xy + c ** 2 * x2 * y2
            return num / jnp.maximum(den, MIN_NORM)

        def _logmap(x, y, c):
            sub = _mobius_add(-x, y, c)
            sub_norm = jnp.maximum(jnp.linalg.norm(sub, axis=-1, keepdims=True), MIN_NORM)
            x2 = jnp.sum(x * x, axis=-1, keepdims=True)
            lam_x = 2.0 / jnp.maximum(1.0 - c * x2, MIN_NORM)
            sqrt_c = jnp.sqrt(c)
            arg = jnp.clip(sqrt_c * sub_norm, 0.0, TANH_CLIP)
            return 2.0 / (sqrt_c * lam_x) * jnp.arctanh(arg) * sub / sub_norm

        def _expmap(x, v, c):
            v_norm = jnp.maximum(jnp.linalg.norm(v, axis=-1, keepdims=True), MIN_NORM)
            x2 = jnp.sum(x * x, axis=-1, keepdims=True)
            lam_x = 2.0 / jnp.maximum(1.0 - c * x2, MIN_NORM)
            sqrt_c = jnp.sqrt(c)
            second = jnp.tanh(sqrt_c * lam_x * v_norm / 2.0) * v / (sqrt_c * v_norm)
            return _mobius_add(x, second, c)
        key = jax.random.key(seed)
        k1, k2, k3 = jax.random.split(key, 3)
        N, C_IN, C_OUT = (1536, 64, 64)
        x = jax.random.normal(k1, (N, C_IN), dtype=jnp.float32) * 0.03
        adj = (jax.random.uniform(k2, (N, N)) < 0.02).astype(jnp.float32)
        bound = 1.0 / np.sqrt(C_IN)
        weight = jax.random.uniform(k3, (C_IN, C_OUT), dtype=jnp.float32, minval=-bound, maxval=bound)
        bias = jnp.zeros((C_OUT,), dtype=jnp.float32)
        return {'x': x, 'adj': adj, 'weight': weight, 'bias': bias}
    _L1_gnn_all = _L1_gnn_setup()
    _L1_gnn_in = {k: v for k, v in _L1_gnn_all.items() if k in ('weight', 'bias', )}
    del _L1_gnn_all

    def _L2_gnn_setup():
        import jax, jax.numpy as jnp
        import numpy as np
        N, D_IN, D_OUT = (16384, 64, 64)
        AVG_DEG = 32.0
        L2_EPS = 1e-12
        key = jax.random.key(seed)
        kx, ka, kw, kb = jax.random.split(key, 4)
        X = jax.random.normal(kx, (N, D_IN), dtype=jnp.float32)
        adj = (jax.random.uniform(ka, (N, N)) < AVG_DEG / N).astype(jnp.float32)
        bound = 1.0 / np.sqrt(2 * D_IN)
        W = jax.random.uniform(kw, (2 * D_IN, D_OUT), dtype=jnp.float32, minval=-bound, maxval=bound)
        b = jax.random.uniform(kb, (D_OUT,), dtype=jnp.float32, minval=-bound, maxval=bound)
        return {'X': X, 'adj': adj, 'W': W, 'b': b}
    _L2_gnn_all = _L2_gnn_setup()
    _L2_gnn_in = {k: v for k, v in _L2_gnn_all.items() if k in ('W', 'b', )}
    del _L2_gnn_all

    def _L3_gnn_setup():
        import jax, jax.numpy as jnp
        import numpy as np
        N, D_IN, D_OUT = (8192, 64, 64)
        MAX_NEIGH = 100
        DECAY = 0.5
        key = jax.random.key(seed)
        k1, k2, k3, k4 = jax.random.split(key, 4)
        stdv = 1.0 / np.sqrt(D_OUT)
        inputs = {'input': jax.random.normal(k1, (N, D_IN), dtype=jnp.float32), 'adj': jax.random.randint(k2, (N, N), 0, 2).astype(jnp.float32), 'weight': jax.random.uniform(k3, (D_IN, D_OUT), minval=-stdv, maxval=stdv, dtype=jnp.float32), 'bias': jax.random.uniform(k4, (D_OUT,), minval=-stdv, maxval=stdv, dtype=jnp.float32)}
        return inputs
    _L3_gnn_all = _L3_gnn_setup()
    _L3_gnn_in = {k: v for k, v in _L3_gnn_all.items() if k in ('weight', 'bias', )}
    del _L3_gnn_all

    return {
        "x": x,
        "adj": adj,
        "L0_gnn_W": _L0_gnn_in["W"],
        "L1_gnn_weight": _L1_gnn_in["weight"],
        "L1_gnn_bias": _L1_gnn_in["bias"],
        "L2_gnn_W": _L2_gnn_in["W"],
        "L2_gnn_b": _L2_gnn_in["b"],
        "L3_gnn_weight": _L3_gnn_in["weight"],
        "L3_gnn_bias": _L3_gnn_in["bias"],
    }

def reference(x, adj, L0_gnn_W, L1_gnn_weight, L1_gnn_bias, L2_gnn_W, L2_gnn_b, L3_gnn_weight, L3_gnn_bias):
    import jax
    import jax.numpy as jnp
    def _L0_gnn_ref(features, adj, W):
        import jax, jax.numpy as jnp
        import numpy as np
        N = 16384
        F_IN = 64
        F_OUT = 64
        neigh = jnp.matmul(adj, features)
        deg = jnp.sum(adj, axis=1, keepdims=True) + 1.0
        neigh = neigh / deg
        data = jnp.concatenate([features, neigh], axis=-1)
        return jnp.matmul(data, W.T)

    def _L1_gnn_ref(x, adj, weight, bias):
        import jax, jax.numpy as jnp
        import numpy as np
        CURV = 1.0
        MIN_NORM = 1e-15
        TANH_CLIP = 1.0 - 1e-05

        def _mobius_add(x, y, c):
            x2 = jnp.sum(x * x, axis=-1, keepdims=True)
            y2 = jnp.sum(y * y, axis=-1, keepdims=True)
            xy = jnp.sum(x * y, axis=-1, keepdims=True)
            num = (1.0 + 2.0 * c * xy + c * y2) * x + (1.0 - c * x2) * y
            den = 1.0 + 2.0 * c * xy + c ** 2 * x2 * y2
            return num / jnp.maximum(den, MIN_NORM)

        def _logmap(x, y, c):
            sub = _mobius_add(-x, y, c)
            sub_norm = jnp.maximum(jnp.linalg.norm(sub, axis=-1, keepdims=True), MIN_NORM)
            x2 = jnp.sum(x * x, axis=-1, keepdims=True)
            lam_x = 2.0 / jnp.maximum(1.0 - c * x2, MIN_NORM)
            sqrt_c = jnp.sqrt(c)
            arg = jnp.clip(sqrt_c * sub_norm, 0.0, TANH_CLIP)
            return 2.0 / (sqrt_c * lam_x) * jnp.arctanh(arg) * sub / sub_norm

        def _expmap(x, v, c):
            v_norm = jnp.maximum(jnp.linalg.norm(v, axis=-1, keepdims=True), MIN_NORM)
            x2 = jnp.sum(x * x, axis=-1, keepdims=True)
            lam_x = 2.0 / jnp.maximum(1.0 - c * x2, MIN_NORM)
            sqrt_c = jnp.sqrt(c)
            second = jnp.tanh(sqrt_c * lam_x * v_norm / 2.0) * v / (sqrt_c * v_norm)
            return _mobius_add(x, second, c)
        c = CURV
        deg = jnp.maximum(adj.sum(axis=1, keepdims=True), 1e-08)
        w = adj / deg
        log_ij = _logmap(x[:, None, :], x[None, :, :], c)
        agg = jnp.einsum('ij,ijc->ic', w, log_ij)
        transformed = agg @ weight + bias
        origin = jnp.zeros_like(transformed)
        return _expmap(origin, transformed, c)

    def _L2_gnn_ref(X, adj, W, b):
        import jax, jax.numpy as jnp
        import numpy as np
        N, D_IN, D_OUT = (16384, 64, 64)
        AVG_DEG = 32.0
        L2_EPS = 1e-12
        deg = jnp.clip(jnp.sum(adj, axis=1, keepdims=True) + 1.0, 1.0, None)
        h_neigh = (adj @ X + X) / deg
        concat = jnp.concatenate([X, h_neigh], axis=1)
        z = concat @ W + b
        out = jax.nn.relu(z)
        norm = jnp.linalg.norm(out, axis=1, keepdims=True)
        return out / jnp.maximum(norm, L2_EPS)

    def _L3_gnn_ref(input, adj, weight, bias):
        import jax, jax.numpy as jnp
        import numpy as np
        N, D_IN, D_OUT = (8192, 64, 64)
        MAX_NEIGH = 100
        DECAY = 0.5
        support = input @ weight
        mask = (adj != 0).astype(support.dtype)
        rank = jnp.cumsum(mask, axis=1)
        deg = rank[:, -1:]
        k = jnp.minimum(deg, float(MAX_NEIGH))
        pos = rank - (deg - k)
        w = mask * jnp.where(pos > 0, DECAY ** (k - pos), 0.0)
        out = w @ support + bias
        return out

    x = _layernorm(x + _L0_gnn_ref(x, adj, L0_gnn_W), axis=-1)
    x = _layernorm(x + _L1_gnn_ref(x, adj, L1_gnn_weight, L1_gnn_bias), axis=-1)
    x = _layernorm(x + _L2_gnn_ref(x, adj, L2_gnn_W, L2_gnn_b), axis=-1)
    x = _layernorm(x + _L3_gnn_ref(x, adj, L3_gnn_weight, L3_gnn_bias), axis=-1)
    return x


_drawn_inputs = setup_inputs


def setup_inputs(seed=0):
    import zlib

    import numpy as np

    out = dict(_drawn_inputs(seed))
    spreads = {'L1_gnn_bias': (0.0, 0.1)}
    factors = {'L2_gnn_b': 2.956}
    for name, (base, spread) in spreads.items():
        noise = np.random.default_rng([zlib.crc32(name.encode()), seed]).standard_normal(out[name].shape)
        drawn = base * np.exp(spread * noise) if base else spread * noise
        out[name] = jnp.asarray(drawn.astype(out[name].dtype))
    for name, factor in factors.items():
        out[name] = (out[name] * factor).astype(out[name].dtype)
    return out
```

```python
import concourse.bass as bass
from concourse import mybir
from contextlib import ExitStack
import numpy as np

P = 128
N = 3327
NT = (N + P - 1) // P
NPAD = NT * P
C = 64
CA = C + 1
CW = 4
W = CW * P
CHUNKS = [(t, min(CW, NT - t)) for t in range(0, NT, CW)]
NC = len(CHUNKS)
NQ = NT // 2
SPLIT = 3
MAX_NEIGH = 100
LN_EPS = 1e-5
MIN_NORM = 1e-15
TANH_CLIP = 1.0 - 1e-05
LN_FLOOR = 1e-18
AB = W // CA
NB1 = (NT + AB - 1) // AB
OFF_ID, OFF_TRI, OFF_W0, OFF_W2 = 0, P, 2 * P, 2 * P + C
OFF_B1, OFF_B2, OFF_B3 = OFF_W2 + C, OFF_W2 + 2 * C, OFF_W2 + 3 * C
OFF_W1, OFF_W3 = OFF_B3 + C, OFF_B3 + 2 * C
NPAR = OFF_W3 + C
KG = C + 2
RING = 8
MR = 8
SR = 3
WR = 4


def adj_resnorm_program(nc, adjT, xin, params, out):
    f32, bf16 = mybir.dt.float32, mybir.dt.bfloat16
    u8, i16 = mybir.dt.uint8, mybir.dt.int16
    ALU, ACT, AX = mybir.AluOpType, mybir.ActivationFunctionType, mybir.AxisListType.X

    PAIRS = [(J, I, min(CW, NT - I)) for J in range(NT) for I in range(J, NT, CW)]
    NP_ = len(PAIRS)
    STAGE_FIRST = {J: min(k for k, p in enumerate(PAIRS) if p[0] == J) for J in range(NT)}
    STAGE_LAST = {J: max(k for k, p in enumerate(PAIRS) if p[0] == J) for J in range(NT)}

    LOADS = [("c", c, q) for c in range(NC) for q in range(NQ)]
    L1_BASE = len(LOADS)
    LOADS += [("p", k, 0) for k in range(NP_)]
    L2_BASE = len(LOADS)
    LOADS += [("c", c, q) for c in range(NC) for q in range(NQ)]

    def lower(k):
        return 1 if PAIRS[k][0] == PAIRS[k][1] else 0

    ARRIVE, count = [], [0] * RING
    for n, (kind, k, _) in enumerate(LOADS):
        count[n % RING] += 32 if kind == "p" and lower(k) < PAIRS[k][2] else 16
        ARRIVE.append(count[n % RING])

    HUSE = [("s", 0), ("s", 1)]
    for s in range(NP_ + 2):
        if s < NP_ and STAGE_FIRST[PAIRS[s][0]] == s and PAIRS[s][0] + 2 < NT:
            HUSE.append(("s", PAIRS[s][0] + 2))
        if 0 <= s - 2 and lower(s - 2) < PAIRS[s - 2][2]:
            HUSE.append(("h", s - 2))
    HB = {use: 6 + i % 2 for i, use in enumerate(HUSE)}

    ctx = ExitStack()
    with ctx:
        def sb(name, shape, dt=f32):
            return ctx.enter_context(nc.sbuf_tensor(name, shape, dt))

        def sem(name):
            return ctx.enter_context(nc.semaphore(name))

        def wait(eng, s, v):
            if v > 0:
                eng.wait_ge(s, v)

        par = sb("par", [P, NPAR])
        XA = sb("XA", [P, NT, CA])
        XB = sb("XB", [P, NT, CA])
        w8 = sb("w8", [P, NT, NPAD], u8)
        ring = sb("ring", [P, RING, 2 * W])
        gramM = sb("gramM", [KG, NPAD])
        gramF = sb("gramF", [P, NT, 2, KG])
        gramS = sb("gramS", [KG, SR, 2, P])
        scratch = sb("scratch", [P, 17, W])
        pb = sb("pb", [P, 2 * W + AB * P])
        tri = sb("tri", [P, P], bf16)
        neg = sb("neg", [P, P], bf16)
        s3 = (gramF[:, :, :, :].rearrange("p t a k -> p (t a k)")[:, 0:NT * SPLIT * C // 2].bitcast(bf16)
              .rearrange("p (t s c) -> p t s c", s=SPLIT, c=C))
        small = sb("small", [P, 16, NT])
        cst = sb("cst", [P, 4])
        PS = ctx.enter_context(nc.psum_tensor("PS", [P, 8, W], f32))

        ident = par[:, OFF_ID:OFF_ID + P]
        b_all = lambda off, nt: par[:, off:off + C].unsqueeze(1).to_broadcast([P, nt, C])
        deg, dcl, rdeg0, rdeg2, x2, Bv, coef, Bc, n2, nrm, mean, var, std, rstd, sdot, Av = (
            small[:, i, :] for i in range(16))
        d2b = [scratch[:, i, :] for i in (0, 1)]
        rb = [scratch[:, i, :] for i in (2, 3, 4)]
        tb = [scratch[:, i, :] for i in (5, 6)]
        lpb = [scratch[:, i, :] for i in (7, 8)]
        lmb = [scratch[:, i, :] for i in (9, 10)]
        hb = [scratch[:, i, :] for i in (11, 12)]
        kdb = [scratch[:, i, :] for i in (13, 14)]
        ktb = [scratch[:, i, :] for i in (15, 16)]
        maskb = [scratch[:, i, :].bitcast(bf16).rearrange("p (j w) -> p j w", j=2) for i in range(3)]
        runb = [scratch[:, 3 + i // 2, (i % 2) * W // 2:(i % 2 + 1) * W // 2].bitcast(bf16) for i in range(MR)]
        WB = NT * P // 2
        wide = [scratch[:, :, :].rearrange("p a w -> p (a w)")[:, i * WB:(i + 1) * WB].bitcast(i16)
                .rearrange("p (j w) -> p j w", j=NT) for i in range(WR)]
        widebf = [scratch[:, :, :].rearrange("p a w -> p (a w)")[:, i * WB:(i + 1) * WB].bitcast(bf16)
                  .rearrange("p (j w) -> p j w", j=NT) for i in range(WR)]
        cat = pb[:, 0:W].rearrange("p (t c) -> p t c", c=2 * C)
        catT = pb[:, W:2 * W]
        yb = pb[:, 2 * W:2 * W + W // 2].rearrange("p (t c) -> p t c", c=C)
        sq = pb[:, 2 * W + W // 2:3 * W].rearrange("p (t c) -> p t c", c=C)
        rf = pb[:, 3 * W:3 * W + CW * KG].rearrange("p (t c) -> p t c", c=KG)
        P1 = pb[:, 0:AB * C].rearrange("p (t c) -> p t c", c=C)
        P2 = pb[:, W:W + AB * C].rearrange("p (t c) -> p t c", c=C)
        aggT = pb[0:C, 2 * W:2 * W + AB * P]
        sqall = scratch[:, :, :].rearrange("p a w -> p (a w)")[:, 0:NT * C].rearrange("p (t c) -> p t c", c=C)

        s_par, s_x, s_out = sem("s_par"), sem("s_x"), sem("s_out")
        s_ld = [sem(f"s_ld{i}") for i in range(RING)]
        s_cst = sem("s_cst")
        s_dve = sem("s_dve")
        s_mask, s_run, s_w8 = sem("s_mask"), sem("s_run"), sem("s_w8")
        S_ = {st: {n: sem(f"{n}{st}") for n in ("tile", "accread", "cat", "tp", "catT", "z", "var", "std", "new",
                                                 "xT", "xTc", "sup")} for st in (0, 2)}
        s_d2, s_D, s_relu, s_v, s_r, s_a, s_l, s_L, s_h, s_hT, s_kd, s_kt, s_agg = (
            sem("q_" + n) for n in ("d2", "D", "relu", "v", "r", "a", "l", "L", "h", "hT", "kd", "kt", "agg"))
        s_sT, s_sc, s_t, s_lv, s_go1 = sem("s_sT"), sem("s_sc"), sem("q_t"), sem("q_lv"), sem("s_go1")
        s_pagg, s_pT, s_pTc, s_pz, s_pzr, s_n2, s_nrm, s_th, s_v1, s_sd1, s_x1 = (
            sem("p_" + n) for n in ("agg", "T", "Tc", "z", "zr", "n2", "nrm", "th", "var", "std", "x1"))
        s_wdv, s_wac, s_l3, s_y3, s_v3, s_sd3, s_o3 = (sem("t_" + n) for n in ("wdv", "wac", "l3", "y", "var", "std", "o"))

        block = ctx.enter_context(nc.Block())

        def bc(ap, nt, c=C):
            return ap.unsqueeze(2).to_broadcast([P, nt, c])

        slot = lambda n: ring[:, n % RING, :]

        WACT = [I for I in range(NT) if I % 3 == 2]
        WDVE = [I for I in range(NT) if I % 3 != 2]
        G3 = CHUNKS

        @block.sync
        def _(sp):
            sp.dma_start(par[:, :], params).then_inc(s_par, 16)
            sp.dma_start(XA[:, :, 0:C], xin).then_inc(s_x, 16)
            for n, (kind, k, q) in enumerate(LOADS):
                m = n - RING
                if m >= 0:
                    mk, mi, mq = LOADS[m]
                    if mk == "p":
                        wait(sp, s_kd, mi + 1)
                        wait(sp, s_kt, min(mi + 1, NP_ - 1))
                    elif m < L1_BASE:
                        wait(sp, s_mask, m + 1)
                        wait(sp, S_[0]["tile"], 2 * m + 2)
                    else:
                        wait(sp, S_[2]["tile"], 2 * (m - L2_BASE) + 2)
                if kind == "c":
                    I0, nt = CHUNKS[k]
                    J0 = NT - 2 - 2 * q
                    dst = slot(n).rearrange("p (j w) -> p j w", j=2)[:, :, 0:nt * P]
                    src = adjT[J0 * P:(J0 + 2) * P, I0 * P:(I0 + nt) * P].rearrange("(j p) w -> p j w", p=P)
                    sp.dma_start(dst, src).then_inc(s_ld[n % RING], 16)
                else:
                    J, I0, nt = PAIRS[k]
                    sp.dma_start(slot(n)[:, 0:nt * P],
                                 adjT[J * P:(J + 1) * P, I0 * P:(I0 + nt) * P]).then_inc(s_ld[n % RING], 16)
                    lo = lower(k)
                    if lo < nt:
                        dst = slot(n)[:, W + lo * P:W + nt * P].rearrange("p (b f) -> p b f", f=P)
                        src = adjT[(I0 + lo) * P:(I0 + nt) * P, J * P:(J + 1) * P].rearrange("(b p) f -> p b f", p=P)
                        sp.dma_start(dst, src).then_inc(s_ld[n % RING], 16)
            for g, (I0, nt) in enumerate(G3):
                wait(sp, s_o3, g + 1)
                sp.dma_start(out[:, I0:I0 + nt, :], XA[:, I0:I0 + nt, 0:C]).then_inc(s_out, 16)
            wait(sp, s_out, 16 * len(G3))

        def arrived(eng, n):
            wait(eng, s_ld[n % RING], ARRIVE[n])

        def tiles():
            for c in range(NC):
                for u in range(NT):
                    yield c * NT + u, c, u, NT - 1 - u

        @block.gpsimd
        def _(pool):
            nc.gpsimd.memset(neg[:, :], -1.0)
            nc.gpsimd.memset(cst[:, 0:1], LN_EPS)
            nc.gpsimd.memset(cst[:, 1:2], LN_FLOOR)
            nc.gpsimd.memset(cst[:, 2:3], -float(2 * P - MAX_NEIGH))
            nc.gpsimd.memset(XA[:, :, C:CA], 1.0).then_inc(s_cst, 1)
            for s in range(NP_ + 3):
                k = s - 1
                if 0 <= k < NP_:
                    w = PAIRS[k][2] * P
                    wait(pool, s_l, k + 1)
                    nc.gpsimd.tensor_tensor(lpb[k % 2][:, 0:w], lpb[k % 2][:, 0:w], lmb[k % 2][:, 0:w],
                                       ALU.subtract).then_inc(s_L, 1)
                k = s - 2
                if 0 <= k < NP_:
                    w = PAIRS[k][2] * P
                    wait(pool, s_h, k + 1)
                    arrived(pool, L1_BASE + k)
                    wait(pool, s_agg, k - 1)
                    nc.gpsimd.tensor_tensor(kdb[k % 2][:, 0:w], hb[k % 2][:, 0:w], slot(L1_BASE + k)[:, 0:w],
                                       ALU.mult).then_inc(s_kd, 1)

        @block.vector
        def _(dve):
            chain = [0]

            def link(ins):
                chain[0] += 1
                ins.then_inc(s_dve, 1)
                dve.wait_ge(s_dve, chain[0])

            v = nc.vector

            def norm_first(y, s, lo, hi, done):
                nt = hi - lo
                link(v.reduce_sum(mean[:, lo:hi], y, AX))
                link(v.tensor_scalar(mean[:, lo:hi], mean[:, lo:hi], 1.0 / C, None, ALU.mult))
                link(v.tensor_tensor(y, y, bc(mean[:, lo:hi], nt), ALU.subtract))
                link(v.tensor_tensor(s, y, y, ALU.mult))
                v.reduce_sum(var[:, lo:hi], s, AX).then_inc(done, 1)

            def norm_last(y, dst, lo, hi):
                link(v.reciprocal(rstd[:, lo:hi], std[:, lo:hi]))
                return v.tensor_tensor(dst, y, bc(rstd[:, lo:hi], hi - lo), ALU.mult)

            def post_a(st, c):
                I0, nt = CHUNKS[c]
                hi = I0 + nt
                q = S_[st]
                X = (XA if st == 0 else XA)[:, I0:hi, 0:C]
                wait(dve, q["tile"], (c + 1) * NT)
                if st == 0:
                    acc = PS[:, c % 2, 0:nt * CA].rearrange("p (t c) -> p t c", c=CA)
                    link(v.tensor_copy(deg[:, I0:hi].unsqueeze(2), acc[:, :, C:CA]))
                    link(v.tensor_scalar(rdeg0[:, I0:hi], deg[:, I0:hi], 1.0, None, ALU.add))
                    link(v.tensor_scalar(rdeg2[:, I0:hi], rdeg0[:, I0:hi], 1.0, None, ALU.max))
                    link(v.reciprocal(rdeg0[:, I0:hi], rdeg0[:, I0:hi]))
                    link(v.reciprocal(rdeg2[:, I0:hi], rdeg2[:, I0:hi]))
                    link(v.tensor_tensor(cat[:, 0:nt, C:2 * C], acc[:, :, 0:C], bc(rdeg0[:, I0:hi], nt), ALU.mult))
                else:
                    acc = PS[:, c % 2, 0:nt * C].rearrange("p (t c) -> p t c", c=C)
                    link(v.tensor_tensor(cat[:, 0:nt, C:2 * C], acc, X, ALU.add))
                    link(v.tensor_tensor(cat[:, 0:nt, C:2 * C], cat[:, 0:nt, C:2 * C], bc(rdeg2[:, I0:hi], nt), ALU.mult))
                v.tensor_copy(cat[:, 0:nt, 0:C], X).then_inc(q["cat"], 1)

            def post_b(st, c):
                I0, nt = CHUNKS[c]
                hi = I0 + nt
                q = S_[st]
                X = XA[:, I0:hi, 0:C]
                y, s = yb[:, 0:nt, :], sq[:, 0:nt, :]
                z = PS[:, 6, 0:nt * C].rearrange("p (t c) -> p t c", c=C)
                wait(dve, q["z"], c + 1)
                if st == 0:
                    link(v.tensor_tensor(y, z, X, ALU.add))
                else:
                    link(v.tensor_tensor(y, z, b_all(OFF_B2, nt), ALU.add))
                    link(v.tensor_scalar(y, y, 0.0, None, ALU.max))
                    link(v.tensor_tensor(s, y, y, ALU.mult))
                    v.reduce_sum(n2[:, I0:hi], s, AX).then_inc(s_n2, 1)
                    wait(dve, s_nrm, 1 + c + 1)
                    link(v.tensor_scalar(nrm[:, I0:hi], nrm[:, I0:hi], 1e-12, None, ALU.max))
                    link(v.reciprocal(nrm[:, I0:hi], nrm[:, I0:hi]))
                    link(v.tensor_tensor(y, y, bc(nrm[:, I0:hi], nt), ALU.mult))
                    link(v.tensor_tensor(y, y, X, ALU.add))
                norm_first(y, s, I0, hi, q["var"])

            def post_c(st, c):
                I0, nt = CHUNKS[c]
                hi = I0 + nt
                q = S_[st]
                y, s = yb[:, 0:nt, :], sq[:, 0:nt, :]
                new = XB[:, I0:hi, 0:C]
                wait(dve, q["std"], c + 1)
                if st == 2:
                    norm_last(y, new, I0, hi).then_inc(q["new"], 1)
                    return
                link(norm_last(y, new, I0, hi))
                link(v.tensor_tensor(s, new, new, ALU.mult))
                link(v.reduce_sum(x2[:, I0:hi], s, AX))
                x2c = x2[:, I0:hi].unsqueeze(2)
                wait(dve, q["xT"], c)
                v.tensor_scalar(XB[:, I0:hi, C:CA], x2c, 1.0, None, ALU.add)
                v.tensor_copy(rf[:, 0:nt, 0:C], new)
                v.tensor_copy(rf[:, 0:nt, C:C + 1], x2c)
                v.memset(rf[:, 0:nt, C + 1:KG], 1.0).then_inc(q["new"], 1)
                for a in (0, 1):
                    v.tensor_scalar(gramF[:, I0:hi, a, 0:C], new, -2.0, None, ALU.mult)
                    v.tensor_copy(gramF[:, I0:hi, a, C + a:C + a + 1], x2c)
                    last = v.memset(gramF[:, I0:hi, a, C + 1 - a:C + 2 - a], 1.0)
                link(last)

            def support(c):
                I0, nt = CHUNKS[c]
                wait(dve, S_[2]["sup"], c + 1)
                z = PS[:, 4, 0:nt * C].rearrange("p (t c) -> p t c", c=C)
                y, s = yb[:, 0:nt, :], sq[:, 0:nt, :]
                sc = float(2 ** (127 - MAX_NEIGH))
                link(v.tensor_scalar(y, z, sc, None, ALU.mult))
                link(v.tensor_copy(s3[:, I0:I0 + nt, 0, :], y))
                link(v.tensor_tensor(s, y, s3[:, I0:I0 + nt, 0, :], ALU.subtract))
                link(v.tensor_copy(s3[:, I0:I0 + nt, 1, :], s))
                v.tensor_tensor(s3[:, I0:I0 + nt, 2, :], s, s3[:, I0:I0 + nt, 1, :],
                                ALU.subtract).then_inc(s_x1, 1)

            wait(dve, s_par, 16)
            v.tensor_copy(tri[:, :], par[:, OFF_TRI:OFF_TRI + P]).then_inc(s_cst, 1)

            def hooks(st, c, q):
                if c < 0:
                    return
                if q == 1:
                    post_a(st, c)
                if q == 6:
                    post_b(st, c)
                if q == 7:
                    post_c(st, c)
                if q == 10 and st == 2:
                    support(c)

            def mask(g):
                c, q = divmod(g, NQ)
                w = CHUNKS[c][1] * P
                arrived(dve, g)
                wait(dve, S_[0]["tile"], 2 * (g - 3) + 2)
                v.tensor_scalar(maskb[g % 3][:, :, 0:w],
                                slot(g).rearrange("p (j w) -> p j w", j=2)[:, :, 0:w],
                                0.0, None, ALU.not_equal).then_inc(s_mask, 1)

            NG = NC * NQ
            mask(0)
            for g in range(NG):
                c, q = divmod(g, NQ)
                w = CHUNKS[c][1] * P
                if g + 1 < NG:
                    mask(g + 1)
                wait(dve, s_mask, g + 1)
                t = 2 * g
                m = maskb[g % 3]
                if q > 0:
                    link(v.tensor_tensor(runb[(t + 1) % MR][:, 0:w], runb[t % MR][:, 0:w], m[:, 1, 0:w], ALU.add))
                    last = v.tensor_tensor(runb[(t + 2) % MR][:, 0:w], runb[(t + 1) % MR][:, 0:w], m[:, 0, 0:w], ALU.add)
                else:
                    last = v.tensor_tensor(runb[(t + 2) % MR][:, 0:w], m[:, 1, 0:w], m[:, 0, 0:w], ALU.add)
                last.then_inc(s_run, 1)
                wait(dve, s_run, g + 1)
                hooks(0, c - 1, q)
            for q in range(NQ):
                hooks(0, NC - 1, q)

            link(v.tensor_scalar(dcl[:, :], deg[:, :], 1e-8, None, ALU.max))
            link(v.reciprocal(dcl[:, :], dcl[:, :]))
            link(v.tensor_scalar(Bv[:, :], x2[:, :], -1.0, 1.0, ALU.mult, ALU.add))
            link(v.tensor_scalar(coef[:, :], Bv[:, :], MIN_NORM, 0.5, ALU.max, ALU.mult))
            link(v.tensor_tensor(coef[:, :], coef[:, :], dcl[:, :], ALU.mult))
            v.tensor_tensor(Bc[:, :], Bv[:, :], coef[:, :], ALU.mult).then_inc(s_go1, 1)
            for s in range(NP_ + 3):
                k = s - 1
                if 0 <= k < NP_:
                    w = PAIRS[k][2] * P
                    wait(dve, s_r, k + 1)
                    wait(dve, s_l, k - 1)
                    v.tensor_tensor(tb[k % 2][:, 0:w], d2b[k % 2][:, 0:w], rb[k % 3][:, 0:w], ALU.mult).then_inc(s_t, 1)
                    wait(dve, s_t, k + 1)
                    v.tensor_scalar(tb[k % 2][:, 0:w], tb[k % 2][:, 0:w], TANH_CLIP, None, ALU.min).then_inc(s_a, 1)
                k = s
                if k < NP_:
                    w = PAIRS[k][2] * P
                    wait(dve, s_D, k + 1)
                    wait(dve, s_relu, k + 1)
                    v.scalar_tensor_tensor(rb[k % 3][:, 0:w], PS[:, 4, 0:w], MIN_NORM, d2b[k % 2][:, 0:w],
                                           ALU.max, ALU.mult).then_inc(s_v, 1)
                k = s - 2
                if 0 <= k < NP_:
                    w = PAIRS[k][2] * P
                    wait(dve, s_L, k + 1)
                    wait(dve, s_kd, k - 1)
                    wait(dve, s_hT, k - 1)
                    v.tensor_tensor(hb[k % 2][:, 0:w], lpb[k % 2][:, 0:w], rb[k % 3][:, 0:w], ALU.mult).then_inc(s_h, 1)
                k = s - 3
                if 0 <= k < NP_ - 1:
                    nt, lo = PAIRS[k][2], lower(k)
                    wait(dve, s_hT, k + 1)
                    arrived(dve, L1_BASE + k)
                    wait(dve, s_agg, k - 1)
                    v.tensor_tensor(ktb[k % 2][:, lo * P:nt * P], PS[:, HB[("h", k)], lo * P:nt * P],
                                    slot(L1_BASE + k)[:, W + lo * P:W + nt * P], ALU.mult).then_inc(s_kt, 1)
            for b in range(NB1):
                lo, hi = b * AB, min(NT, b * AB + AB)
                nt = hi - lo
                acc = PS[:, b, 0:nt * CA].rearrange("p (t c) -> p t c", c=CA)
                V, U = acc[:, :, 0:C], acc[:, :, C:CA]
                X = XB[:, lo:hi, 0:C]
                p1, p2 = P1[:, 0:nt, :], P2[:, 0:nt, :]
                wait(dve, s_agg, STAGE_LAST[hi - 1] + 1)
                wait(dve, s_pT, 2 * b)
                link(v.tensor_tensor(p1, V, X, ALU.mult))
                link(v.reduce_sum(sdot[:, lo:hi], p1, AX))
                link(v.scalar_tensor_tensor(Av[:, lo:hi].unsqueeze(2), sdot[:, lo:hi].unsqueeze(2), -2.0, U, ALU.mult, ALU.add))
                link(v.tensor_tensor(Av[:, lo:hi], Av[:, lo:hi], coef[:, lo:hi], ALU.mult))
                link(v.tensor_tensor(p1, X, bc(Av[:, lo:hi], nt), ALU.mult))
                link(v.tensor_tensor(p2, V, bc(Bc[:, lo:hi], nt), ALU.mult))
                v.tensor_tensor(p2, p2, p1, ALU.subtract).then_inc(s_pagg, 1)
                wait(dve, s_pz, b + 1)
                z = PS[:, b, 0:nt * C].rearrange("p (t c) -> p t c", c=C)
                link(v.tensor_tensor(XA[:, lo:hi, 0:C], z, b_all(OFF_B1, nt), ALU.add))
                link(v.tensor_tensor(p1, XA[:, lo:hi, 0:C], XA[:, lo:hi, 0:C], ALU.mult))
                link(v.reduce_sum(n2[:, lo:hi], p1, AX))
            v.tensor_scalar(n2[:, :], n2[:, :], 0.0, None, ALU.max).then_inc(s_n2, 1)
            Y = XA[:, :, 0:C]
            wait(dve, s_nrm, 1)
            v.tensor_scalar(nrm[:, :], nrm[:, :], MIN_NORM, None, ALU.max).then_inc(s_v1, 1)
            wait(dve, s_v1, 1)
            link(v.reciprocal(Av[:, :], nrm[:, :]))
            wait(dve, s_th, 1)
            link(v.tensor_tensor(Av[:, :], Av[:, :], sdot[:, :], ALU.mult))
            link(v.tensor_tensor(Y, Y, bc(Av[:, :], NT), ALU.mult))
            link(v.tensor_tensor(Y, Y, XB[:, :, 0:C], ALU.add))
            norm_first(Y, sqall, 0, NT, s_v1)
            wait(dve, s_sd1, 1)
            norm_last(Y, Y, 0, NT).then_inc(s_x1, 1)

            done_w = [0]

            def widen(I):
                wait(dve, s_l3, I - WR + 1)
                v.tensor_scalar(wide[I % WR], w8[:, :, I * P:(I + 1) * P], float(P), None,
                                ALU.mult).then_inc(s_wdv, 1)

            for I in WDVE:
                if I < WR:
                    widen(I)
            for c in range(NC):
                for q in range(NQ):
                    hooks(2, c, q)
            todo = [I for I in WDVE if I >= WR]
            for g, (I0, nt) in enumerate(G3):
                hi = I0 + nt
                while todo and todo[0] < hi + WR:
                    widen(todo.pop(0))
                y, s = yb[:, 0:nt, :], sq[:, 0:nt, :]
                wait(dve, s_o3, g)
                wait(dve, s_l3, hi)
                for i in range(I0, hi, 2):
                    part = PS[:, (i // 2) % 4, 0:2 * SPLIT * C].rearrange("p (t s c) -> p t c s", s=SPLIT, c=C)
                    last = v.tensor_reduce(y[:, i - I0:i - I0 + 2, :], part, AX, ALU.add)
                last.then_inc(s_y3, 1)
                wait(dve, s_y3, g + 1)
                link(v.tensor_tensor(y, y, XB[:, I0:hi, 0:C], ALU.add))
                link(v.tensor_tensor(y, y, b_all(OFF_B3, nt), ALU.add))
                norm_first(y, s, I0, hi, s_v3)
                wait(dve, s_sd3, g + 1)
                norm_last(y, XA[:, I0:hi, 0:C], I0, hi).then_inc(s_o3, 1)

        @block.scalar
        def _(act):
            a = nc.scalar

            def copy_catT(st, c):
                nt = CHUNKS[c][1]
                wait(act, S_[st]["tp"], c + 1)
                a.copy(catT[:, 0:nt * P], PS[:, 5, 0:nt * P]).then_inc(S_[st]["catT"], 1)

            def deviation(lo, hi, ready, n, done):
                wait(act, ready, n)
                a.activation(std[:, lo:hi], var[:, lo:hi], ACT.Sqrt, bias=cst[:, 0:1], scale=1.0 / C).then_inc(done, 1)

            def norm_std(st, c):
                I0, nt = CHUNKS[c]
                if st == 2:
                    wait(act, s_n2, 1 + c + 1)
                    a.activation(nrm[:, I0:I0 + nt], n2[:, I0:I0 + nt], ACT.Sqrt).then_inc(s_nrm, 1)
                deviation(I0, I0 + nt, S_[st]["var"], c + 1, S_[st]["std"])

            def copy_xT(st, c):
                I0, nt = CHUNKS[c]
                wait(act, S_[st]["xT"], c + 1)
                rows = KG if st == 0 else C
                a.copy(gramM[0:rows, I0 * P:(I0 + nt) * P], PS[0:rows, 7, 0:nt * P]).then_inc(S_[st]["xTc"], 1)

            def hooks(st, c, u):
                if c < 0:
                    return
                if u == 9:
                    copy_catT(st, c)
                if u == 14:
                    norm_std(st, c)
                if u == 20:
                    copy_xT(st, c)

            wait(act, s_cst, 2)
            for t, c, u, J in tiles():
                I0, nt = CHUNKS[c]
                wait(act, S_[0]["tile"], t + 1)
                a.activation(w8[:, J, I0 * P:(I0 + nt) * P], PS[:, 2 + t % 3, 0:nt * P], ACT.Relu,
                             bias=cst[:, 2:3]).then_inc(s_w8, 1)
                hooks(0, c - 1, u)
            for u in range(NT):
                hooks(0, NC - 1, u)

            def s_copy(J):
                wait(act, s_sT, J + 1)
                a.copy(gramS[:, J % SR, :, :].rearrange("k a p -> k (a p)"),
                       PS[0:KG, HB[("s", J)], 0:2 * P]).then_inc(s_sc, 1)

            s_copy(0)
            s_copy(1)
            for s in range(NP_ + 1):
                k = s
                if k < NP_:
                    w = PAIRS[k][2] * P
                    wait(act, s_d2, k + 1)
                    wait(act, s_a, k - 1)
                    a.activation(d2b[k % 2][:, 0:w], PS[:, 5, 0:w], ACT.Relu).then_inc(s_relu, 1)
                k = s - 1
                if 0 <= k:
                    w = PAIRS[k][2] * P
                    wait(act, s_a, k + 1)
                    wait(act, s_h, k - 1)
                    a.activation(lpb[k % 2][:, 0:w], tb[k % 2][:, 0:w], ACT.Ln, bias=1.0)
                    a.activation(lmb[k % 2][:, 0:w], tb[k % 2][:, 0:w], ACT.Ln, bias=1.0, scale=-1.0).then_inc(s_l, 1)
                k = s
                if k < NP_:
                    J = PAIRS[k][0]
                    w = PAIRS[k][2] * P
                    wait(act, s_v, k + 1)
                    a.activation(rb[k % 3][:, 0:w], rb[k % 3][:, 0:w], ACT.Ln, bias=cst[:, 1:2]).then_inc(s_lv, 1)
                    wait(act, s_lv, k + 1)
                    a.activation(rb[k % 3][:, 0:w], rb[k % 3][:, 0:w], ACT.Exp, scale=-0.5).then_inc(s_r, 1)
                    if STAGE_FIRST[J] == k and J + 2 < NT:
                        s_copy(J + 2)
            for b in range(NB1):
                lo, hi = b * AB, min(NT, b * AB + AB)
                nt = hi - lo
                for r in range(2):
                    i0, i1 = 4 * r, min(nt, 4 * r + 4)
                    wait(act, s_pT, 2 * b + r + 1)
                    a.copy(aggT[:, i0 * P:i1 * P], PS[0:C, b, 0:(i1 - i0) * P]).then_inc(s_pTc, 1)
            wait(act, s_n2, 1)
            a.activation(nrm[:, :], n2[:, :], ACT.Sqrt).then_inc(s_nrm, 1)
            wait(act, s_v1, 1)
            a.activation(sdot[:, :], nrm[:, :], ACT.Tanh).then_inc(s_th, 1)
            deviation(0, NT, s_v1, 2, s_sd1)

            def widen(I):
                wait(act, s_l3, I - WR + 1)
                a.activation(wide[I % WR], w8[:, :, I * P:(I + 1) * P], ACT.Copy, scale=float(P)).then_inc(s_wac, 1)

            wait(act, s_x1, 1)
            for I in WACT:
                if I < WR:
                    widen(I)
            for c in range(NC):
                for u in range(NT):
                    hooks(2, c, u)
            todo = [I for I in WACT if I >= WR]
            for g, (I0, nt) in enumerate(G3):
                while todo and todo[0] < I0 + nt + WR:
                    widen(todo.pop(0))
                deviation(I0, I0 + nt, s_v3, g + 1, s_sd3)

        @block.tensor
        def _(pe):
            T = nc.tensor

            def transposes(st, c):
                nt = CHUNKS[c][1]
                wait(pe, S_[st]["cat"], c + 1)
                wait(pe, S_[st]["catT"], c)
                for i in range(nt):
                    last = T.transpose(PS[:, 5, i * P:(i + 1) * P], cat[:, i, :], ident)
                last.then_inc(S_[st]["tp"], 1)

            def project(st, c):
                nt = CHUNKS[c][1]
                wait(pe, S_[st]["catT"], c + 1)
                wait(pe, S_[st]["var"], c)
                off = OFF_W0 if st == 0 else OFF_W2
                for i in range(nt):
                    last = T.matmul(PS[:, 6, i * C:(i + 1) * C], catT[:, i * P:(i + 1) * P],
                                    par[:, off:off + C], start=True, stop=True)
                last.then_inc(S_[st]["z"], 1)

            def x_transposes(st, c):
                I0, nt = CHUNKS[c]
                wait(pe, S_[st]["new"], c + 1)
                wait(pe, S_[st]["xTc"], c)
                for i in range(nt):
                    src = rf[:, i, :] if st == 0 else XB[:, I0 + i, 0:C]
                    rows = KG if st == 0 else C
                    last = T.transpose(PS[0:rows, 7, i * P:(i + 1) * P], src, ident)
                last.then_inc(S_[st]["xT"], 1)

            def supports(c):
                I0, nt = CHUNKS[c]
                wait(pe, S_[2]["xTc"], c + 1)
                wait(pe, s_x1, 1 + c)
                for i in range(nt):
                    t = I0 + i
                    last = T.matmul(PS[:, 4, i * C:(i + 1) * C], gramM[0:C, t * P:(t + 1) * P],
                                    par[0:C, OFF_W3:OFF_W3 + C], start=True, stop=True)
                last.then_inc(S_[2]["sup"], 1)

            def hooks(st, c, u):
                if c < 0:
                    return
                if u == 7:
                    transposes(st, c)
                if u == 10:
                    project(st, c)
                if u == 17:
                    x_transposes(st, c)
                if u == 21 and st == 2:
                    supports(c)

            def stream(st, base):
                q = S_[st]
                ca = CA if st == 0 else C
                for t, c, u, J in tiles():
                    g, nt = t // 2, CHUNKS[c][1]
                    w = nt * P
                    jj = J % 2
                    arrived(pe, base + g)
                    if u == 0:
                        wait(pe, q["cat"], c - 1)
                    for i in range(nt):
                        last = T.matmul(PS[:, c % 2, i * ca:(i + 1) * ca],
                                        slot(base + g)[:, jj * W + i * P:jj * W + (i + 1) * P],
                                        XA[:, J, 0:ca], start=(u == 0 and i == 0), stop=(u == NT - 1),
                                        skip_group_check=True)
                    if st == 0:
                        bank = PS[:, 2 + t % 3, 0:w]
                        wait(pe, s_mask, g + 1)
                        wait(pe, s_w8, t - 2)
                        last = T.matmul(bank, tri[:, :], maskb[g % 3][:, jj, 0:w], start=True, stop=(u == 0))
                        if u == 1:
                            last = T.matmul(bank, neg[:, :], maskb[g % 3][:, 1, 0:w], start=False, stop=True)
                        elif u > 1:
                            wait(pe, s_run, g if u % 2 == 0 else g + 1)
                            last = T.matmul(bank, neg[:, :], runb[t % MR][:, 0:w], start=False, stop=True)
                    last.then_inc(q["tile"], 1)
                    hooks(st, c - 1, u)
                for u in range(NT):
                    hooks(st, NC - 1, u)

            wait(pe, s_par, 16)
            wait(pe, s_x, 16)
            wait(pe, s_cst, 2)
            stream(0, 0)

            def s_transposes(J):
                bank = HB[("s", J)]
                release(("s", J))
                wait(pe, s_sc, J - SR + 1)
                for v_ in (0, 1):
                    last = T.transpose(PS[0:KG, bank, v_ * P:(v_ + 1) * P], gramF[:, J, v_, :], ident)
                last.then_inc(s_sT, 1)

            def release(use):
                n = HUSE.index(use)
                if n >= 2:
                    kind, i = HUSE[n - 2]
                    wait(pe, s_sc if kind == "s" else s_kt, i + 1)

            def gram(k):
                J, I0, nt = PAIRS[k]
                w = nt * P
                if STAGE_FIRST[J] == k:
                    wait(pe, s_sc, J + 1)
                mv = gramM[:, I0 * P:I0 * P + w]
                wait(pe, s_relu, k)
                T.matmul(PS[:, 5, 0:w], gramS[:, J % SR, 1, :], mv, start=True, stop=True).then_inc(s_d2, 1)
                wait(pe, s_v, k)
                T.matmul(PS[:, 4, 0:w], gramS[:, J % SR, 0, :], mv, start=True, stop=True).then_inc(s_D, 1)

            wait(pe, S_[0]["xTc"], NC)
            wait(pe, s_w8, NC * NT)
            wait(pe, s_go1, 1)
            s_transposes(0)
            s_transposes(1)
            gram(0)
            for s in range(NP_ + 3):
                if s < NP_:
                    J = PAIRS[s][0]
                    if STAGE_FIRST[J] == s and J + 2 < NT:
                        s_transposes(J + 2)
                if s + 1 < NP_:
                    gram(s + 1)
                k = s - 2
                if 0 <= k < NP_:
                    nt, lo = PAIRS[k][2], lower(k)
                    wait(pe, s_h, k + 1)
                    if lo < nt:
                        release(("h", k))
                        for i in range(lo, nt):
                            last = T.transpose(PS[:, HB[("h", k)], i * P:(i + 1) * P], hb[k % 2][:, i * P:(i + 1) * P], ident)
                        last.then_inc(s_hT, 1)
                k = s - 3
                if 0 <= k < NP_:
                    J, I0, nt = PAIRS[k]
                    lo = lower(k)
                    wait(pe, s_kd, k + 1)
                    for i in range(nt):
                        I = I0 + i
                        last = T.matmul(PS[:, I // AB, (I % AB) * CA:(I % AB + 1) * CA], kdb[k % 2][:, i * P:(i + 1) * P],
                                        XB[:, J, :], start=(J == 0 and I % AB == 0), stop=(J == NT - 1),
                                        skip_group_check=True)
                    if lo < nt:
                        wait(pe, s_kt, k + 1)
                    for i in range(lo, nt):
                        last = T.matmul(PS[:, J // AB, (J % AB) * CA:(J % AB + 1) * CA], ktb[k % 2][:, i * P:(i + 1) * P],
                                        XB[:, I0 + i, :], start=False, stop=False, skip_group_check=True)
                    last.then_inc(s_agg, 1)
            for b in range(NB1):
                lo, hi = b * AB, min(NT, b * AB + AB)
                nt = hi - lo
                wait(pe, s_pagg, b + 1)
                for r in range(2):
                    if r == 1:
                        wait(pe, s_pTc, 2 * b + 1)
                    for i in range(4 * r, min(nt, 4 * r + 4)):
                        last = T.transpose(PS[0:C, b, (i % 4) * P:(i % 4 + 1) * P], P2[:, i, :], ident)
                    last.then_inc(s_pT, 1)
                wait(pe, s_pTc, 2 * b + 2)
                for i in range(nt):
                    last = T.matmul(PS[:, b, i * C:(i + 1) * C], aggT[:, i * P:(i + 1) * P],
                                    par[0:C, OFF_W1:OFF_W1 + C], start=True, stop=True)
                last.then_inc(s_pz, 1)

            wait(pe, s_x1, 1)
            stream(2, L2_BASE)

            wait(pe, s_x1, 1 + NC)
            for I in range(NT):
                if I in WACT:
                    wait(pe, s_wac, WACT.index(I) + 1)
                else:
                    wait(pe, s_wdv, WDVE.index(I) + 1)
                b = (I // 2) % 4
                if I % CW == 0:
                    wait(pe, s_y3, I // CW - 1)
                for J in range(NT):
                    o = (I % 2) * SPLIT * C
                    last = T.matmul(PS[:, b, o:o + SPLIT * C], widebf[I % WR][:, J, :],
                                    s3[:, J, :, :].rearrange("p s c -> p (s c)"),
                                    start=(J == 0 and I % 2 == 0), stop=(J == NT - 1), skip_group_check=True)
                last.then_inc(s_l3, 1)


_INPUTS = ("adjT", "xin", "params")


def kernel(x, adj, L0_gnn_W, L1_gnn_weight, L1_gnn_bias, L2_gnn_W, L2_gnn_b, L3_gnn_weight, L3_gnn_bias):
    import concourse.bacc as bacc
    from concourse.bass_utils import run_bass_kernel_spmd

    pad = NPAD - N
    adjT = np.ascontiguousarray(np.pad(np.asarray(adj).T, ((0, pad), (0, pad))))
    xin = np.ascontiguousarray(np.pad(np.asarray(x), ((0, pad), (0, 0))).reshape(NT, P, C).transpose(1, 0, 2))
    tri = (2.0 * P * np.eye(P) - np.tril(np.ones((P, P)), -1)).astype(np.float32)
    rows = lambda b: np.broadcast_to(np.asarray(b), (P, C))
    tall = lambda w: np.pad(np.asarray(w), ((0, P - C), (0, 0)))
    params = np.ascontiguousarray(np.concatenate(
        [np.eye(P, dtype=np.float32), tri, np.asarray(L0_gnn_W).T, np.asarray(L2_gnn_W),
         rows(L1_gnn_bias), rows(L2_gnn_b), rows(L3_gnn_bias), tall(L1_gnn_weight), tall(L3_gnn_weight)], axis=1))
    arrays = {"adjT": adjT, "xin": xin, "params": params}

    nc = bacc.Bacc("TRN2", target_bir_lowering=False, num_devices=1)
    args = [nc.dram_tensor(n, arrays[n].shape, mybir.dt.float32, kind="ExternalInput").ap() for n in _INPUTS]
    out = nc.dram_tensor("out", (P, NT, C), mybir.dt.float32, kind="ExternalOutput").ap()
    adj_resnorm_program(nc, *args, out)
    r = run_bass_kernel_spmd(nc, [arrays], core_ids=[0])
    y = np.asarray(r.results[0]["out"])
    return np.ascontiguousarray(y.transpose(1, 0, 2).reshape(NPAD, C)[:N])
```

```python
import concourse.bass as bass
from concourse import mybir
from contextlib import ExitStack
import numpy as np

P = 128
N = 3327
NT = (N + P - 1) // P
NPAD = NT * P
C = 64
CA = C + 1
CW = 4
W = CW * P
CHUNKS = [(t, min(CW, NT - t)) for t in range(0, NT, CW)]
NC = len(CHUNKS)
NQ = NT // 2
SPLIT = 3
MAX_NEIGH = 100
LN_EPS = 1e-5
MIN_NORM = 1e-15
TANH_CLIP = 1.0 - 1e-05
LN_FLOOR = 1e-18
OFF_ID, OFF_TRI = 0, P
(OFF_W0X, OFF_W0N, OFF_W2X, OFF_W2N, OFF_B1, OFF_B2, OFF_B3, OFF_W1, OFF_W3,
 NPAR) = (2 * P + i * C for i in range(10))
KG = C + 2
DVE_Q = (3, 7, 11)
POOL_Q = tuple(q for q in range(NQ) if q not in DVE_Q)
RING = 8
MK = 5
MR = 2 * MK
WR = 4


def adj_resnorm_program(nc, adjT, xin, xTin, params, out):
    f32, bf16 = mybir.dt.float32, mybir.dt.bfloat16
    u8, i16 = mybir.dt.uint8, mybir.dt.int16
    ALU, ACT, AX = mybir.AluOpType, mybir.ActivationFunctionType, mybir.AxisListType.X

    PAIRS = [(A, J, min(nt, J - I0 + 1), min(nt, J - I0)) for A, (I0, nt) in enumerate(CHUNKS) for J in range(I0, NT)]
    NP_ = len(PAIRS)
    FIRST = [min(k for k, p in enumerate(PAIRS) if p[0] == A) for A in range(NC)]
    LAST = [max(k for k, p in enumerate(PAIRS) if p[0] == A) for A in range(NC)]
    MIRRORS = [sum(1 for p in PAIRS[:k + 1] if p[3]) for k in range(NP_)]
    FLUSH = [(A, max(t, I0 + 1), min(t + CW, NT)) for A, (I0, _) in enumerate(CHUNKS) for t in range(I0, NT, CW)]
    FLUSH_AT = [max(k for k, p in enumerate(PAIRS) if p[0] == A and p[1] < hi) for A, lo, hi in FLUSH]
    FLUSH_OF = {(p[0], p[1]): min(f for f in range(len(FLUSH)) if FLUSH_AT[f] >= k) for k, p in enumerate(PAIRS)}

    SIDE = [(FLUSH_AT[f] + 4, 0, f) for f in range(len(FLUSH))]
    for A in range(NC):
        turns = (4, 5, 6, 8, 9, 10, 11) if A < NC - 3 else (4, 4, 5, 5, 5, 6, 7)
        SIDE += [(LAST[A] + turn, 1 + i, A) for i, turn in enumerate(turns)]
        if A + 1 < NC:
            SIDE += [(FIRST[A] + 1 + i, 8 + i, A + 1) for i in range(3)]
    SIDE.sort()
    LOOP = NP_ + 3

    def side_work(s, steps):
        for turn, step, c in SIDE:
            if step in steps and (turn == s or (s == LOOP - 1 and turn > s)):
                steps[step](c)

    LOADS = [("c", c, q) for c in range(NC) for q in range(NQ)]
    L1_BASE = len(LOADS)
    LOADS += [("p", k, 0) for k in range(NP_)]
    L2_BASE = len(LOADS)
    LOADS += [("c", c, q) for c in range(NC) for q in range(NQ)]

    ARRIVE, count = [], [0] * RING
    for n, (kind, k, _) in enumerate(LOADS):
        count[n % RING] += 32 if kind == "p" and PAIRS[k][3] else 16
        ARRIVE.append(count[n % RING])

    HUSE = [("m", 0), ("m", 1)]
    for s in range(LOOP):
        if 0 <= s - 2 < NP_ and PAIRS[s - 2][3]:
            HUSE.append(("h", s - 2))
        side_work(s, {9: lambda A: HUSE.extend([("m", 2 * A), ("m", 2 * A + 1)])})
    HB = {use: 6 + i % 2 for i, use in enumerate(HUSE)}

    ctx = ExitStack()
    with ctx:
        def sb(name, shape, dt=f32):
            return ctx.enter_context(nc.sbuf_tensor(name, shape, dt))

        def sem(name):
            return ctx.enter_context(nc.semaphore(name))

        def wait(eng, s, v):
            if v > 0:
                eng.wait_ge(s, v)

        par = sb("par", [P, NPAR])
        XA = sb("XA", [P, NT, CA])
        XB = sb("XB", [P, NT, CA])
        w8 = sb("w8", [P, NT, NPAD], u8)
        ring = sb("ring", [P, RING, 2 * W])
        gramM = sb("gramM", [KG, NPAD])
        gramX = sb("gramX", [P, 2, 2, W])
        mirror = sb("mirror", [P, NPAD])
        scratch = sb("scratch", [P, 15, W])
        pb = sb("pb", [P, 2 * CW * C + 2 * CW * KG + CW * CA])
        tri = sb("tri", [P, P], bf16)
        neg = sb("neg", [P, P], bf16)
        s3 = (mirror[:, 0:NT * SPLIT * C // 2].bitcast(bf16)
              .rearrange("p (t s c) -> p t s c", s=SPLIT, c=C))
        small = sb("small", [P, 16, NT])
        cst = sb("cst", [P, 4])
        one = cst[:, 3:4]
        PS = ctx.enter_context(nc.psum_tensor("PS", [P, 8, W], f32))

        ident = par[:, OFF_ID:OFF_ID + P]
        b_all = lambda off, nt: par[:, off:off + C].unsqueeze(1).to_broadcast([P, nt, C])
        deg, dcl, rdeg0, rdeg2, x2, Bv, coef, Bc, n2, nrm, mean, var, std, rstd, sdot, Av = (
            small[:, i, :] for i in range(16))
        d2b = [scratch[:, i, :] for i in (0, 1)]
        rb = [scratch[:, i, :] for i in (2, 3, 4)]
        tb = d2b
        lpb = [scratch[:, i, :] for i in (5, 6)]
        lmb = [scratch[:, i, :] for i in (7, 8)]
        hb = [scratch[:, i, :] for i in (9, 10)]
        kdb = [scratch[:, i, :] for i in (11, 12)]
        ktb = [scratch[:, i, :] for i in (13, 14)]
        maskb = [scratch[:, i, :].bitcast(bf16).rearrange("p (j w) -> p j w", j=2) for i in (0, 1, 2, 11, 12)]
        runb = [scratch[:, (3, 4, 5, 6, 13)[i // 2], (i % 2) * W // 2:(i % 2 + 1) * W // 2].bitcast(bf16) for i in range(MR)]
        sum_pool = [gramX[:, i, :, :].rearrange("p a w -> p (a w)") for i in (0, 1)]
        sum_dve = [scratch[:, i:i + 2, :].rearrange("p a w -> p (a w)") for i in (7, 9)]
        WB = NT * P // 2
        wide = [scratch[:, :, :].rearrange("p a w -> p (a w)")[:, i * WB:(i + 1) * WB].bitcast(i16)
                .rearrange("p (j w) -> p j w", j=NT) for i in range(WR)]
        widebf = [scratch[:, :, :].rearrange("p a w -> p (a w)")[:, i * WB:(i + 1) * WB].bitcast(bf16)
                  .rearrange("p (j w) -> p j w", j=NT) for i in range(WR)]
        accT = mirror[:, NPAD - W:NPAD]
        yb = pb[:, 0:CW * C].rearrange("p (t c) -> p t c", c=C)
        sq = pb[:, CW * C:2 * CW * C].rearrange("p (t c) -> p t c", c=C)
        rf = pb[:, 2 * CW * C:2 * CW * C + 2 * CW * KG].rearrange("p (t a c) -> p t a c", a=2, c=KG)
        pv = pb[:, 2 * CW * C + 2 * CW * KG:].rearrange("p (t c) -> p t c", c=CA)
        sqall = scratch[:, :, :].rearrange("p a w -> p (a w)")[:, 0:NT * C].rearrange("p (t c) -> p t c", c=C)

        s_par, s_x, s_xTin, s_out = sem("s_par"), sem("s_x"), sem("s_xTin"), sem("s_out")
        s_ld = [sem(f"s_ld{i}") for i in range(RING)]
        s_cst = sem("s_cst")
        s_dve, s_act = sem("s_dve"), sem("s_act")
        s_mask, s_run, s_odd, s_w8, s_cnt, s_sumd, s_sump, s_sum, s_xT2, s_xT2c = (
            sem("s_" + n) for n in ("mask", "run", "odd", "w8", "cnt", "sumd", "sump", "sum", "xT2", "xT2c"))
        S_ = {st: {n: sem(f"{n}{st}") for n in ("grp", "accT", "z", "var", "std", "feat", "new", "xT", "xTc",
                                                 "sup")} for st in (0, 2)}
        s_d2, s_D, s_relu, s_v, s_r, s_a, s_l, s_L, s_h, s_hT, s_kd, s_kt, s_agg = (
            sem("q_" + n) for n in ("d2", "D", "relu", "v", "r", "a", "l", "L", "h", "hT", "kd", "kt", "agg"))
        s_mT, s_mc, s_rf, s_t, s_lv, s_go1, s_fl = (sem("q_" + n) for n in ("mT", "mc", "rf", "t", "lv", "go1", "fl"))
        s_pacc, s_prow, s_pagg, s_pT, s_pTc, s_pz, s_pzr, s_n2, s_nrm, s_th, s_v1, s_sd1, s_x1 = (
            sem("p_" + n) for n in ("acc", "row", "agg", "T", "Tc", "z", "zr", "n2", "nrm", "th", "var", "std", "x1"))
        s_wdv, s_wac, s_l3, s_y3, s_v3, s_sd3, s_o3 = (sem("t_" + n) for n in ("wdv", "wac", "l3", "y", "var", "std", "o"))

        block = ctx.enter_context(nc.Block())

        def bc(ap, nt, c=C):
            return ap.unsqueeze(2).to_broadcast([P, nt, c])

        slot = lambda n: ring[:, n % RING, :]

        WACT = [I for I in range(NT) if I % 3 == 2]
        WDVE = [I for I in range(NT) if I % 3 != 2]
        G3 = CHUNKS

        def summed(g):
            c, q = divmod(g, NQ)
            if q in POOL_Q:
                return s_sump, c * (len(POOL_Q) - 1) + max(POOL_Q.index(q), 1)
            return s_sumd, c * len(DVE_Q) + DVE_Q.index(q) + 1

        @block.sync
        def _(sp):
            sp.dma_start(XA[:, :, 0:C], xin).then_inc(s_x, 16)
            sp.dma_start(par[:, :], params).then_inc(s_par, 16)
            for n, (kind, k, q) in enumerate(LOADS):
                if n == RING:
                    sp.dma_start(gramM[0:C, :], xTin).then_inc(s_xTin, 16)
                m = n - RING
                if m >= 0:
                    mk, mi, mq = LOADS[m]
                    if mk == "p":
                        wait(sp, s_kd, mi + 1)
                        wait(sp, s_kt, MIRRORS[mi])
                    elif m < L1_BASE:
                        wait(sp, s_mask, m + 1)
                        wait(sp, S_[0]["grp"], m + 1)
                        wait(sp, *summed(m))
                    else:
                        wait(sp, S_[2]["grp"], m - L2_BASE + 1)
                if kind == "c":
                    I0, nt = CHUNKS[k]
                    J0 = NT - 2 - 2 * q
                    dst = slot(n).rearrange("p (j w) -> p j w", j=2)[:, :, 0:nt * P]
                    src = adjT[J0 * P:(J0 + 2) * P, I0 * P:(I0 + nt) * P].rearrange("(j p) w -> p j w", p=P)
                    sp.dma_start(dst, src).then_inc(s_ld[n % RING], 16)
                else:
                    A, J, nb, nm = PAIRS[k]
                    I0 = CHUNKS[A][0]
                    sp.dma_start(slot(n)[:, 0:nb * P],
                                 adjT[J * P:(J + 1) * P, I0 * P:(I0 + nb) * P]).then_inc(s_ld[n % RING], 16)
                    if nm:
                        dst = slot(n)[:, W:W + nm * P].rearrange("p (b f) -> p b f", f=P)
                        src = adjT[I0 * P:(I0 + nm) * P, J * P:(J + 1) * P].rearrange("(b p) f -> p b f", p=P)
                        sp.dma_start(dst, src).then_inc(s_ld[n % RING], 16)
            for g, (I0, nt) in enumerate(G3):
                wait(sp, s_o3, g + 1)
                sp.dma_start(out[:, I0:I0 + nt, :], XA[:, I0:I0 + nt, 0:C]).then_inc(s_out, 16)
            wait(sp, s_out, 16 * len(G3))

        def arrived(eng, n):
            wait(eng, s_ld[n % RING], ARRIVE[n])

        def tiles():
            for c in range(NC):
                for u in range(NT):
                    yield c * NT + u, c, u, NT - 1 - u

        @block.gpsimd
        def _(pool):
            nc.gpsimd.memset(neg[:, :], -1.0)
            nc.gpsimd.memset(cst[:, 0:1], LN_EPS)
            nc.gpsimd.memset(cst[:, 1:2], LN_FLOOR)
            nc.gpsimd.memset(cst[:, 2:3], -float(2 * P - MAX_NEIGH))
            nc.gpsimd.memset(one, 1.0).then_inc(s_cst, 1)
            for c in range(NC):
                w = CHUNKS[c][1] * P
                both = sum_pool[c % 2][:, 0:2 * w]
                load = lambda q: slot(c * NQ + q).rearrange("p (j w) -> p j w", j=2)[:, :, 0:w]
                sums = both.rearrange("p (j w) -> p j w", j=2)
                arrived(pool, c * NQ)
                wait(pool, s_sum, c - 1)
                for q in POOL_Q[1:]:
                    arrived(pool, c * NQ + q)
                    nc.gpsimd.tensor_tensor(sums, load(0) if q == 1 else sums, load(q), ALU.add).then_inc(s_sump, 1)
                    wait(pool, *summed(c * NQ + q))
            for s in range(NP_ + 3):
                k = s - 1
                if 0 <= k < NP_:
                    w = PAIRS[k][2] * P
                    wait(pool, s_l, k + 1)
                    nc.gpsimd.tensor_tensor(lpb[k % 2][:, 0:w], lpb[k % 2][:, 0:w], lmb[k % 2][:, 0:w],
                                       ALU.subtract).then_inc(s_L, 1)
                k = s - 2
                if 0 <= k < NP_:
                    w = PAIRS[k][2] * P
                    wait(pool, s_h, k + 1)
                    arrived(pool, L1_BASE + k)
                    wait(pool, s_agg, k - 1)
                    nc.gpsimd.tensor_tensor(kdb[k % 2][:, 0:w], hb[k % 2][:, 0:w], slot(L1_BASE + k)[:, 0:w],
                                       ALU.mult).then_inc(s_kd, 1)

        @block.vector
        def _(dve):
            chain = [0]

            def link(ins):
                chain[0] += 1
                ins.then_inc(s_dve, 1)
                dve.wait_ge(s_dve, chain[0])

            v = nc.vector

            def centre(y, lo, hi):
                link(v.reduce_sum(mean[:, lo:hi], y, AX))
                link(v.tensor_scalar(mean[:, lo:hi], mean[:, lo:hi], 1.0 / C, None, ALU.mult))
                return v.tensor_tensor(y, y, bc(mean[:, lo:hi], hi - lo), ALU.subtract)

            def norm_first(y, s, lo, hi, done):
                link(centre(y, lo, hi))
                link(v.tensor_tensor(s, y, y, ALU.mult))
                v.reduce_sum(var[:, lo:hi], s, AX).then_inc(done, 1)

            def norm_last(y, dst, lo, hi):
                link(v.reciprocal(rstd[:, lo:hi], std[:, lo:hi]))
                return v.tensor_tensor(dst, y, bc(rstd[:, lo:hi], hi - lo), ALU.mult)

            def column_sums(c):
                w = 2 * CHUNKS[c][1] * P
                wait(dve, s_sumd, (c + 1) * len(DVE_Q))
                wait(dve, s_sump, (c + 1) * (len(POOL_Q) - 1))
                v.tensor_tensor(sum_dve[c % 2][:, 0:w], sum_dve[c % 2][:, 0:w], sum_pool[c % 2][:, 0:w], ALU.add).then_inc(s_sum, 1)

            def post_b(st, c):
                I0, nt = CHUNKS[c]
                hi = I0 + nt
                q = S_[st]
                X = XA[:, I0:hi, 0:C]
                y, s = yb[:, 0:nt, :], sq[:, 0:nt, :]
                z = PS[:, 6, 0:nt * 2 * C].rearrange("p (t a c) -> p t a c", a=2, c=C)
                wait(dve, q["z"], c + 1)
                if st == 0:
                    link(v.tensor_copy(deg[:, I0:hi], PS[:, 5, 0:nt]))
                    link(v.tensor_scalar(rdeg0[:, I0:hi], deg[:, I0:hi], 1.0, None, ALU.add))
                    link(v.tensor_scalar(rdeg2[:, I0:hi], rdeg0[:, I0:hi], 1.0, None, ALU.max))
                    link(v.reciprocal(rdeg0[:, I0:hi], rdeg0[:, I0:hi]))
                    link(v.reciprocal(rdeg2[:, I0:hi], rdeg2[:, I0:hi]))
                    link(v.tensor_tensor(y, z[:, :, 0, :], bc(rdeg0[:, I0:hi], nt), ALU.mult))
                    link(v.tensor_tensor(y, z[:, :, 1, :], y, ALU.add))
                    link(v.tensor_tensor(y, y, X, ALU.add))
                else:
                    link(v.tensor_tensor(y, z[:, :, 0, :], bc(rdeg2[:, I0:hi], nt), ALU.mult))
                    link(v.tensor_tensor(y, z[:, :, 1, :], y, ALU.add))
                    link(v.tensor_tensor(y, y, b_all(OFF_B2, nt), ALU.add))
                    link(v.tensor_scalar(y, y, 0.0, None, ALU.max))
                    link(v.tensor_tensor(s, y, y, ALU.mult))
                    v.reduce_sum(n2[:, I0:hi], s, AX).then_inc(s_n2, 1)
                    wait(dve, s_nrm, 1 + c + 1)
                    link(v.tensor_scalar(nrm[:, I0:hi], nrm[:, I0:hi], 1e-12, None, ALU.max))
                    link(v.reciprocal(nrm[:, I0:hi], nrm[:, I0:hi]))
                    link(v.tensor_tensor(y, y, bc(nrm[:, I0:hi], nt), ALU.mult))
                    link(v.tensor_tensor(y, y, X, ALU.add))
                centre(y, I0, hi).then_inc(q["var"], 1)

            def post_c(st, c):
                I0, nt = CHUNKS[c]
                hi = I0 + nt
                q = S_[st]
                y, s = yb[:, 0:nt, :], sq[:, 0:nt, :]
                new = XB[:, I0:hi, 0:C]
                wait(dve, q["std"], c + 1)
                norm_last(y, new, I0, hi).then_inc(q["feat"], 1)

            def support(c):
                I0, nt = CHUNKS[c]
                wait(dve, S_[2]["sup"], c + 1)
                z = PS[:, 4, 0:nt * C].rearrange("p (t c) -> p t c", c=C)
                y, s = yb[:, 0:nt, :], sq[:, 0:nt, :]
                sc = float(2 ** (127 - MAX_NEIGH))
                link(v.tensor_scalar(y, z, sc, None, ALU.mult))
                link(v.tensor_copy(s3[:, I0:I0 + nt, 0, :], y))
                link(v.tensor_tensor(s, y, s3[:, I0:I0 + nt, 0, :], ALU.subtract))
                link(v.tensor_copy(s3[:, I0:I0 + nt, 1, :], s))
                v.tensor_tensor(s3[:, I0:I0 + nt, 2, :], s, s3[:, I0:I0 + nt, 1, :],
                                ALU.subtract).then_inc(s_x1, 1)

            v.memset(rf[:, :, 0, C + 1:KG], 1.0)
            v.memset(mirror[C:2 * C, 0:P], 0.0)
            wait(dve, s_par, 16)
            v.tensor_copy(tri[:, :], par[:, OFF_TRI:OFF_TRI + P]).then_inc(s_cst, 1)

            def hooks(st, c, q):
                if c < 0:
                    return
                if q == 3 and st == 0:
                    column_sums(c)
                if q == 6:
                    post_b(st, c)
                if q == 8:
                    post_c(st, c)
                if q == 10 and st == 2:
                    support(c)

            def mask(g):
                if g >= NC * NQ:
                    return
                c, q = divmod(g, NQ)
                w = CHUNKS[c][1] * P
                arrived(dve, g)
                wait(dve, s_cnt, 2 * (g - MK) + 2)
                v.tensor_scalar(maskb[g % MK][:, :, 0:w],
                                slot(g).rearrange("p (j w) -> p j w", j=2)[:, :, 0:w],
                                0.0, None, ALU.not_equal).then_inc(s_mask, 1)

            NG = NC * NQ
            mask(0)
            for g in range(NG):
                c, q = divmod(g, NQ)
                w = CHUNKS[c][1] * P
                wait(dve, s_mask, g + 1)
                t = 2 * g
                m = maskb[g % MK]
                wait(dve, s_cnt, t + 3 - MR)
                if q > 0:
                    wait(dve, s_run, g)
                    v.tensor_tensor(runb[(t + 1) % MR][:, 0:w], runb[t % MR][:, 0:w], m[:, 1, 0:w], ALU.add).then_inc(s_odd, 1)
                mask(g + 1)
                if q > 0:
                    wait(dve, s_odd, g - c)
                    last = v.tensor_tensor(runb[(t + 2) % MR][:, 0:w], runb[(t + 1) % MR][:, 0:w], m[:, 0, 0:w], ALU.add)
                else:
                    last = v.tensor_tensor(runb[(t + 2) % MR][:, 0:w], m[:, 1, 0:w], m[:, 0, 0:w], ALU.add)
                last.then_inc(s_run, 1)
                if q in DVE_Q:
                    sums = sum_dve[c % 2][:, 0:2 * w].rearrange("p (j w) -> p j w", j=2)
                    load = slot(g).rearrange("p (j w) -> p j w", j=2)[:, :, 0:w]
                    if q == DVE_Q[0]:
                        wait(dve, S_[0]["z"], c - 1)
                        v.tensor_copy(sums, load).then_inc(s_sumd, 1)
                    else:
                        wait(dve, s_sumd, summed(g)[1] - 1)
                        v.tensor_tensor(sums, sums, load, ALU.add).then_inc(s_sumd, 1)
                hooks(0, c - 1, q)
            for q in range(NQ):
                hooks(0, NC - 1, q)

            wait(dve, S_[0]["new"], NC)
            link(v.tensor_scalar(dcl[:, :], deg[:, :], 1e-8, None, ALU.max))
            link(v.reciprocal(dcl[:, :], dcl[:, :]))
            link(v.tensor_scalar(Bv[:, :], x2[:, :], -1.0, 1.0, ALU.mult, ALU.add))
            link(v.tensor_scalar(coef[:, :], Bv[:, :], MIN_NORM, 0.5, ALU.max, ALU.mult))
            link(v.tensor_tensor(coef[:, :], coef[:, :], dcl[:, :], ALU.mult))
            v.tensor_tensor(Bc[:, :], Bv[:, :], coef[:, :], ALU.mult).then_inc(s_go1, 1)

            def gram_rows(A):
                I0, nt = CHUNKS[A]
                x2c = x2[:, I0:I0 + nt].unsqueeze(2)
                wait(dve, S_[0]["xT"], NC)
                wait(dve, s_mT, 2 * A)
                for a in (0, 1):
                    v.tensor_copy(rf[:, 0:nt, a, 0:C], XB[:, I0:I0 + nt, 0:C])
                    v.tensor_copy(rf[:, 0:nt, a, C + a:C + a + 1], x2c)
                    last = v.memset(rf[:, 0:nt, a, C + 1 - a:C + 2 - a], 1.0)
                last.then_inc(s_rf, 1)

            def flush(f):
                A, lo, hi = FLUSH[f]
                if lo >= hi:
                    return
                wait(dve, s_agg, FLUSH_AT[f] + 1)
                wait(dve, s_fl, f)
                src = PS[C:2 * C, 2 + f % 2, (lo % CW) * P:(lo % CW + hi - lo) * P]
                dst = mirror[C:2 * C, lo * P:hi * P]
                if A == 0:
                    v.tensor_copy(dst, src).then_inc(s_fl, 1)
                else:
                    v.tensor_tensor(dst, src, dst, ALU.add).then_inc(s_fl, 1)

            def aggregate(A):
                lo, nt = CHUNKS[A]
                hi = lo + nt
                X = XB[:, lo:hi, 0:C]
                rows = PS[:, A % 2, 0:nt * P].rearrange("p (t a c) -> p t a c", a=2, c=C)
                V, U = pv[:, 0:nt, 0:C], pv[:, 0:nt, C:CA]
                p1, p2 = yb[:, 0:nt, :], sq[:, 0:nt, :]
                wait(dve, s_prow, A + 1)
                wait(dve, s_pz, A)
                link(v.tensor_copy(pv[:, 0:nt, 1:CA], rows[:, :, 0, :]))
                link(v.tensor_tensor(pv[:, 0:nt, 1:CA], rows[:, :, 1, :], pv[:, 0:nt, 1:CA], ALU.add))
                link(v.tensor_reduce(pv[:, 0:nt, 0:1], pv[:, 0:nt, 1:C], AX, ALU.add, negate=True))
                link(v.tensor_tensor(p1, V, X, ALU.mult))
                link(v.reduce_sum(sdot[:, lo:hi], p1, AX))
                link(v.scalar_tensor_tensor(Av[:, lo:hi].unsqueeze(2), sdot[:, lo:hi].unsqueeze(2), -2.0, U, ALU.mult, ALU.add))
                link(v.tensor_tensor(Av[:, lo:hi], Av[:, lo:hi], coef[:, lo:hi], ALU.mult))
                link(v.tensor_tensor(p1, X, bc(Av[:, lo:hi], nt), ALU.mult))
                link(v.tensor_tensor(p2, V, bc(Bc[:, lo:hi], nt), ALU.mult))
                v.tensor_tensor(p2, p2, p1, ALU.subtract).then_inc(s_pagg, 1)

            def tangent(A):
                lo, nt = CHUNKS[A]
                hi = lo + nt
                z = PS[:, A % 2, 0:nt * C].rearrange("p (t c) -> p t c", c=C)
                wait(dve, s_pz, A + 1)
                link(v.tensor_tensor(XA[:, lo:hi, 0:C], z, b_all(OFF_B1, nt), ALU.add))
                link(v.tensor_tensor(yb[:, 0:nt, :], XA[:, lo:hi, 0:C], XA[:, lo:hi, 0:C], ALU.mult))
                link(v.reduce_sum(n2[:, lo:hi], yb[:, 0:nt, :], AX))
                v.memset(sdot[:, lo:hi], 0.0).then_inc(s_pzr, 1)

            steps = {0: flush, 3: aggregate, 7: tangent, 8: gram_rows}
            gram_rows(0)
            for s in range(LOOP):
                k = s - 1
                if 0 <= k < NP_:
                    w = PAIRS[k][2] * P
                    wait(dve, s_r, k + 1)
                    v.tensor_tensor(tb[k % 2][:, 0:w], d2b[k % 2][:, 0:w], rb[k % 3][:, 0:w], ALU.mult).then_inc(s_t, 1)
                    wait(dve, s_t, k + 1)
                    v.tensor_scalar(tb[k % 2][:, 0:w], tb[k % 2][:, 0:w], TANH_CLIP, None, ALU.min).then_inc(s_a, 1)
                k = s
                if k < NP_:
                    w = PAIRS[k][2] * P
                    wait(dve, s_D, k + 1)
                    wait(dve, s_relu, k + 1)
                    v.scalar_tensor_tensor(rb[k % 3][:, 0:w], PS[:, 4, 0:w], MIN_NORM, d2b[k % 2][:, 0:w],
                                           ALU.max, ALU.mult).then_inc(s_v, 1)
                k = s - 2
                if 0 <= k < NP_:
                    w = PAIRS[k][2] * P
                    wait(dve, s_L, k + 1)
                    wait(dve, s_kd, k - 1)
                    wait(dve, s_hT, MIRRORS[k - 2] if k >= 2 else 0)
                    v.tensor_tensor(hb[k % 2][:, 0:w], lpb[k % 2][:, 0:w], rb[k % 3][:, 0:w], ALU.mult).then_inc(s_h, 1)
                k = s - 3
                if 0 <= k < NP_ and PAIRS[k][3]:
                    wm = PAIRS[k][3] * P
                    wait(dve, s_hT, MIRRORS[k])
                    arrived(dve, L1_BASE + k)
                    wait(dve, s_agg, k - 1)
                    v.tensor_tensor(ktb[k % 2][:, 0:wm], PS[:, HB[("h", k)], 0:wm],
                                    slot(L1_BASE + k)[:, W:W + wm], ALU.mult).then_inc(s_kt, 1)
                side_work(s, steps)
            Y = XA[:, :, 0:C]
            wait(dve, s_nrm, 1)
            v.tensor_scalar(nrm[:, :], nrm[:, :], MIN_NORM, None, ALU.max).then_inc(s_v1, 1)
            wait(dve, s_v1, 1)
            link(v.reciprocal(Av[:, :], nrm[:, :]))
            wait(dve, s_th, 1)
            link(v.tensor_tensor(Av[:, :], Av[:, :], sdot[:, :], ALU.mult))
            link(v.tensor_tensor(Y, Y, bc(Av[:, :], NT), ALU.mult))
            link(v.tensor_tensor(Y, Y, XB[:, :, 0:C], ALU.add))
            norm_first(Y, sqall, 0, NT, s_v1)
            wait(dve, s_sd1, 1)
            norm_last(Y, Y, 0, NT).then_inc(s_x1, 1)

            done_w = [0]

            def widen(I):
                wait(dve, s_l3, I - WR + 1)
                v.tensor_scalar(wide[I % WR], w8[:, :, I * P:(I + 1) * P], float(P), None,
                                ALU.mult).then_inc(s_wdv, 1)

            for I in WDVE:
                if I < WR:
                    widen(I)
            for c in range(NC):
                for q in range(NQ):
                    hooks(2, c, q)
            todo = [I for I in WDVE if I >= WR]
            for g, (I0, nt) in enumerate(G3):
                hi = I0 + nt
                while todo and todo[0] < hi + WR:
                    widen(todo.pop(0))
                y, s = yb[:, 0:nt, :], sq[:, 0:nt, :]
                wait(dve, s_o3, g)
                wait(dve, s_l3, hi)
                for i in range(I0, hi, 2):
                    part = PS[:, (i // 2) % 4, 0:2 * SPLIT * C].rearrange("p (t s c) -> p t c s", s=SPLIT, c=C)
                    last = v.tensor_reduce(y[:, i - I0:i - I0 + 2, :], part, AX, ALU.add)
                last.then_inc(s_y3, 1)
                wait(dve, s_y3, g + 1)
                link(v.tensor_tensor(y, y, XB[:, I0:hi, 0:C], ALU.add))
                link(v.tensor_tensor(y, y, b_all(OFF_B3, nt), ALU.add))
                centre(y, I0, hi).then_inc(s_v3, 1)
                wait(dve, s_sd3, g + 1)
                norm_last(y, XA[:, I0:hi, 0:C], I0, hi).then_inc(s_o3, 1)

        @block.scalar
        def _(act):
            a = nc.scalar

            def copy_accT(st, c):
                nt = CHUNKS[c][1]
                wait(act, S_[st]["grp"], (c + 1) * NQ)
                wait(act, S_[st]["z"], c)
                a.copy(accT[:, 0:nt * P], PS[:, c % 2, 0:nt * P]).then_inc(S_[st]["accT"], 1)

            def deviation(lo, hi, ready, n, done):
                wait(act, ready, n)
                a.activation(std[:, lo:hi], var[:, lo:hi], ACT.Sqrt, bias=cst[:, 0:1], scale=1.0 / C).then_inc(done, 1)

            act_chain = [0]

            def link(ins):
                act_chain[0] += 1
                ins.then_inc(s_act, 1)
                act.wait_ge(s_act, act_chain[0])

            def squares(y, dst, lo, hi):
                for i in range(hi - lo):
                    last = a.activation(sq[:, i, :], y[:, i, :], ACT.Square, accum_out=dst[:, lo + i:lo + i + 1])
                link(last)

            def norm_std(st, c):
                I0, nt = CHUNKS[c]
                if st == 2:
                    wait(act, s_n2, c + 1)
                    a.activation(nrm[:, I0:I0 + nt], n2[:, I0:I0 + nt], ACT.Sqrt).then_inc(s_nrm, 1)
                wait(act, S_[st]["var"], c + 1)
                squares(yb, var, I0, I0 + nt)
                deviation(I0, I0 + nt, S_[st]["var"], c + 1, S_[st]["std"])

            def features(c):
                I0, nt = CHUNKS[c]
                hi = I0 + nt
                wait(act, S_[0]["feat"], c + 1)
                squares(XB[:, I0:hi, 0:C], x2, I0, hi)
                wait(act, S_[0]["xT"], c)
                a.activation(XB[:, I0:hi, C:CA], x2[:, I0:hi].unsqueeze(2), ACT.Identity, bias=1.0)
                a.copy(rf[:, 0:nt, 0, C:C + 1], x2[:, I0:hi].unsqueeze(2))
                a.mul(rf[:, 0:nt, 0, 0:C], XB[:, I0:hi, 0:C], -2.0).then_inc(S_[0]["new"], 1)

            def copy_xT(st, c):
                I0, nt = CHUNKS[c]
                wait(act, S_[st]["xT"], c + 1)
                rows = KG if st == 0 else C
                a.copy(gramM[0:rows, I0 * P:(I0 + nt) * P], PS[0:rows, 7, 0:nt * P]).then_inc(S_[st]["xTc"], 1)

            def hooks(st, c, u):
                if c < 0:
                    return
                if u == 3:
                    copy_accT(st, c)
                if u == 15:
                    norm_std(st, c)
                if u == 18 and st == 0:
                    features(c)
                if u == 22:
                    copy_xT(st, c)

            wait(act, s_cst, 2)
            for t, c, u, J in tiles():
                I0, nt = CHUNKS[c]
                wait(act, s_cnt, t + 1)
                a.activation(w8[:, J, I0 * P:(I0 + nt) * P], PS[:, 2 + t % 3, 0:nt * P], ACT.Relu,
                             bias=cst[:, 2:3]).then_inc(s_w8, 1)
                hooks(0, c - 1, u)
            for u in range(NT):
                hooks(0, NC - 1, u)

            def moving_copy(A):
                nt = CHUNKS[A][1]
                for a_ in (0, 1):
                    use = 2 * A + a_
                    wait(act, s_mT, use + 1)
                    wait(act, s_D, FIRST[A - 1] if A >= 2 else 0)
                    a.copy(gramX[0:KG, A % 2, a_, 0:nt * P], PS[0:KG, HB[("m", use)], 0:nt * P]).then_inc(s_mc, 1)

            def acc_copy(A):
                lo, nt = CHUNKS[A]
                wait(act, s_agg, LAST[A] + 1)
                a.copy(mirror[0:C, lo * P:(lo + nt) * P], PS[0:C, A % 2, 0:nt * P]).then_inc(s_pacc, 1)

            def agg_copy(A):
                lo, nt = CHUNKS[A]
                wait(act, s_pT, A + 1)
                a.copy(mirror[0:C, lo * P:(lo + nt) * P], PS[0:C, A % 2, 0:nt * P]).then_inc(s_pTc, 1)

            steps = {1: acc_copy, 5: agg_copy, 10: moving_copy}
            a.preload_act_table_set("natural_log_exp_and_others")
            moving_copy(0)
            for s in range(LOOP):
                k = s
                if k < NP_:
                    w = PAIRS[k][2] * P
                    wait(act, s_d2, k + 1)
                    wait(act, s_l, k - 1)
                    a.activation(d2b[k % 2][:, 0:w], PS[:, 5, 0:w], ACT.Relu).then_inc(s_relu, 1)
                k = s - 1
                if 0 <= k < NP_:
                    w = PAIRS[k][2] * P
                    wait(act, s_a, k + 1)
                    wait(act, s_h, k - 1)
                    a.activation(lpb[k % 2][:, 0:w], tb[k % 2][:, 0:w], ACT.Ln, bias=1.0)
                    a.activation(lmb[k % 2][:, 0:w], tb[k % 2][:, 0:w], ACT.Ln, bias=1.0, scale=-1.0).then_inc(s_l, 1)
                k = s
                if k < NP_:
                    w = PAIRS[k][2] * P
                    wait(act, s_v, k + 1)
                    a.activation(rb[k % 3][:, 0:w], rb[k % 3][:, 0:w], ACT.Ln, bias=cst[:, 1:2]).then_inc(s_lv, 1)
                    wait(act, s_lv, k + 1)
                    a.activation(rb[k % 3][:, 0:w], rb[k % 3][:, 0:w], ACT.Exp, scale=-0.5).then_inc(s_r, 1)
                side_work(s, steps)
            wait(act, s_pzr, NC)
            a.activation(nrm[:, :], n2[:, :], ACT.Sqrt).then_inc(s_nrm, 1)
            wait(act, s_v1, 1)
            a.activation(sdot[:, :], nrm[:, :], ACT.Tanh).then_inc(s_th, 1)
            deviation(0, NT, s_v1, 2, s_sd1)

            def widen(I):
                wait(act, s_l3, I - WR + 1)
                a.activation(wide[I % WR], w8[:, :, I * P:(I + 1) * P], ACT.Copy, scale=float(P)).then_inc(s_wac, 1)

            wait(act, s_x1, 1)
            for I in WACT:
                if I < WR:
                    widen(I)
            for c in range(NC):
                I0, nt = CHUNKS[c]
                wait(act, s_xT2, c + 1)
                a.copy(gramM[0:C, I0 * P:(I0 + nt) * P], PS[0:C, 7, 0:nt * P]).then_inc(s_xT2c, 1)
            for c in range(NC):
                for u in range(NT):
                    hooks(2, c, u)
            todo = [I for I in WACT if I >= WR]
            for g, (I0, nt) in enumerate(G3):
                while todo and todo[0] < I0 + nt + WR:
                    widen(todo.pop(0))
                wait(act, s_v3, g + 1)
                squares(yb, var, I0, I0 + nt)
                deviation(I0, I0 + nt, s_v3, g + 1, s_sd3)

        @block.tensor
        def _(pe):
            T = nc.tensor

            def project(st, c):
                I0, nt = CHUNKS[c]
                WX, WN = (OFF_W0X, OFF_W0N) if st == 0 else (OFF_W2X, OFF_W2N)
                wait(pe, s_xTin, 16)
                wait(pe, S_[st]["accT"], c + 1)
                wait(pe, S_[st]["var"], c)
                for i in range(nt):
                    o = i * 2 * C
                    cols = slice((I0 + i) * P, (I0 + i + 1) * P)
                    T.matmul(PS[:, 6, o:o + C], accT[:, i * P:(i + 1) * P], par[:, WN:WN + C],
                             start=True, stop=(st == 0))
                    if st == 2:
                        T.matmul(PS[:, 6, o:o + C], gramM[0:C, cols], par[0:C, WN:WN + C], start=False, stop=True)
                    last = T.matmul(PS[:, 6, o + C:o + 2 * C], gramM[0:C, cols], par[0:C, WX:WX + C],
                                    start=True, stop=True)
                if st == 0:
                    wait(pe, s_sum, c + 1)
                    w = nt * P
                    for i in range(nt):
                        T.matmul(PS[:, 5, i:i + 1], sum_dve[c % 2][:, i * P:(i + 1) * P], one, start=True, stop=False)
                        last = T.matmul(PS[:, 5, i:i + 1], sum_dve[c % 2][:, w + i * P:w + (i + 1) * P], one,
                                        start=False, stop=True)
                last.then_inc(S_[st]["z"], 1)

            def x_transposes(st, c):
                I0, nt = CHUNKS[c]
                wait(pe, S_[st]["new" if st == 0 else "feat"], c + 1)
                wait(pe, S_[st]["xTc"], c)
                for i in range(nt):
                    src = rf[:, i, 0, :] if st == 0 else XB[:, I0 + i, 0:C]
                    rows = KG if st == 0 else C
                    last = T.transpose(PS[0:rows, 7, i * P:(i + 1) * P], src, ident)
                last.then_inc(S_[st]["xT"], 1)

            def supports(c):
                I0, nt = CHUNKS[c]
                wait(pe, S_[2]["xTc"], c + 1)
                wait(pe, s_x1, 1 + c)
                for i in range(nt):
                    t = I0 + i
                    last = T.matmul(PS[:, 4, i * C:(i + 1) * C], gramM[0:C, t * P:(t + 1) * P],
                                    par[0:C, OFF_W3:OFF_W3 + C], start=True, stop=True)
                last.then_inc(S_[2]["sup"], 1)

            def hooks(st, c, q):
                if c < 0:
                    return
                if q == 4:
                    project(st, c)
                if q == 10:
                    x_transposes(st, c)
                if q == 11 and st == 2:
                    supports(c)

            def stream(st, base):
                sems = S_[st]
                for g in range(NC * NQ):
                    c, q = divmod(g, NQ)
                    w = CHUNKS[c][1] * P
                    J0 = NT - 2 - 2 * q
                    arrived(pe, base + g)
                    if q == 0:
                        wait(pe, sems["accT"], c - 1)
                    for half, jj in ((0, 1), (1, 0)):
                        last = T.matmul(PS[half * C:(half + 1) * C, c % 2, 0:w], XA[:, J0 + jj, 0:C],
                                        slot(base + g)[:, jj * W:jj * W + w], start=(q == 0), stop=(q == NQ - 1),
                                        skip_group_check=True)
                    last.then_inc(sems["grp"], 1)
                    for u in (2 * q, 2 * q + 1) if st == 0 else ():
                        t, jj = c * NT + u, 1 - u % 2
                        bank = PS[:, 2 + t % 3, 0:w]
                        wait(pe, s_mask, g + 1)
                        wait(pe, s_w8, t - 2)
                        last = T.matmul(bank, tri[:, :], maskb[g % MK][:, jj, 0:w], start=True, stop=(u == 0))
                        if u == 1:
                            last = T.matmul(bank, neg[:, :], maskb[g % MK][:, 1, 0:w], start=False, stop=True)
                        elif u > 1:
                            wait(pe, s_run, g if u % 2 == 0 else g + 1)
                            last = T.matmul(bank, neg[:, :], runb[t % MR][:, 0:w], start=False, stop=True)
                        last.then_inc(s_cnt, 1)
                    if st == 2 and g % 2 == 1 and g // 2 < NC:
                        own_transposes(g // 2)
                    hooks(st, c - 1, q)
                for q in range(NQ):
                    hooks(st, NC - 1, q)

            def own_transposes(c):
                I0, nt = CHUNKS[c]
                wait(pe, s_xT2c, c)
                for i in range(nt):
                    last = T.transpose(PS[0:C, 7, i * P:(i + 1) * P], XA[:, I0 + i, 0:C], ident)
                last.then_inc(s_xT2, 1)

            wait(pe, s_par, 16)
            wait(pe, s_x, 16)
            wait(pe, s_cst, 2)
            stream(0, 0)

            def moving_transposes(A):
                nt = CHUNKS[A][1]
                wait(pe, s_rf, A + 1)
                for a_ in (0, 1):
                    release(("m", 2 * A + a_))
                    for i in range(nt):
                        last = T.transpose(PS[0:KG, HB[("m", 2 * A + a_)], i * P:(i + 1) * P], rf[:, i, a_, :], ident)
                    last.then_inc(s_mT, 1)

            def release(use):
                n = HUSE.index(use)
                if n >= 2:
                    kind, i = HUSE[n - 2]
                    if kind == "m":
                        wait(pe, s_mc, i + 1)
                    else:
                        wait(pe, s_kt, MIRRORS[i])

            def gram(k):
                A, J, nb, _ = PAIRS[k]
                w = nb * P
                G = gramM[:, J * P:(J + 1) * P]
                wait(pe, s_mc, 2 * A + 2)
                wait(pe, s_relu, k)
                T.matmul(PS[:, 5, 0:w], G, gramX[0:KG, A % 2, 1, 0:w], start=True, stop=True).then_inc(s_d2, 1)
                wait(pe, s_v, k)
                T.matmul(PS[:, 4, 0:w], G, gramX[0:KG, A % 2, 0, 0:w], start=True, stop=True).then_inc(s_D, 1)

            def sum_rows(A):
                lo, nt = CHUNKS[A]
                wait(pe, s_pacc, A + 1)
                wait(pe, s_fl, max(f for f in range(len(FLUSH)) if FLUSH[f][0] <= A and FLUSH[f][1] < lo + nt) + 1)
                for i in range(nt):
                    last = T.transpose(PS[:, A % 2, i * P:(i + 1) * P], mirror[:, (lo + i) * P:(lo + i + 1) * P], ident)
                last.then_inc(s_prow, 1)

            def agg_transposes(A):
                wait(pe, s_pagg, A + 1)
                for i in range(CHUNKS[A][1]):
                    last = T.transpose(PS[0:C, A % 2, i * P:(i + 1) * P], sq[:, i, :], ident)
                last.then_inc(s_pT, 1)

            def agg_project(A):
                lo, nt = CHUNKS[A]
                wait(pe, s_pTc, A + 1)
                for i in range(nt):
                    last = T.matmul(PS[:, A % 2, i * C:(i + 1) * C], mirror[0:C, (lo + i) * P:(lo + i + 1) * P],
                                    par[0:C, OFF_W1:OFF_W1 + C], start=True, stop=True)
                last.then_inc(s_pz, 1)

            steps = {2: sum_rows, 4: agg_transposes, 6: agg_project, 9: moving_transposes}
            wait(pe, S_[0]["xTc"], NC)
            wait(pe, s_w8, NC * NT)
            wait(pe, s_go1, 1)
            moving_transposes(0)
            gram(0)
            for s in range(LOOP):
                if s + 1 < NP_:
                    gram(s + 1)
                k = s - 2
                if 0 <= k < NP_:
                    wait(pe, s_h, k + 1)
                    if PAIRS[k][3]:
                        release(("h", k))
                        for i in range(PAIRS[k][3]):
                            last = T.transpose(PS[:, HB[("h", k)], i * P:(i + 1) * P], hb[k % 2][:, i * P:(i + 1) * P], ident)
                        last.then_inc(s_hT, 1)
                k = s - 3
                if 0 <= k < NP_:
                    A, J, nb, nm = PAIRS[k]
                    I0 = CHUNKS[A][0]
                    f = FLUSH_OF[(A, J)]
                    if k == FIRST[A]:
                        wait(pe, s_pzr, A - 1)
                    wait(pe, s_kd, k + 1)
                    if nm:
                        wait(pe, s_kt, MIRRORS[k])
                        wait(pe, s_fl, f - 1)
                    for i in range(nb):
                        last = T.matmul(PS[0:C, A % 2, i * P:(i + 1) * P], XB[:, J, 1:CA], kdb[k % 2][:, i * P:(i + 1) * P],
                                        start=(k == FIRST[A] and i == 0), stop=(J == NT - 1), skip_group_check=True)
                        if i < nm:
                            last = T.matmul(PS[C:2 * C, 2 + f % 2, (J % CW) * P:(J % CW + 1) * P], XB[:, I0 + i, 1:CA],
                                            ktb[k % 2][:, i * P:(i + 1) * P], start=(J == FLUSH[f][1] and i == 0),
                                            stop=(i == nm - 1), skip_group_check=True)
                    last.then_inc(s_agg, 1)
                side_work(s, steps)

            wait(pe, s_x1, 1)
            stream(2, L2_BASE)

            wait(pe, s_x1, 1 + NC)
            for I in range(NT):
                if I in WACT:
                    wait(pe, s_wac, WACT.index(I) + 1)
                else:
                    wait(pe, s_wdv, WDVE.index(I) + 1)
                b = (I // 2) % 4
                if I % CW == 0:
                    wait(pe, s_y3, I // CW - 1)
                for J in range(NT):
                    o = (I % 2) * SPLIT * C
                    last = T.matmul(PS[:, b, o:o + SPLIT * C], widebf[I % WR][:, J, :],
                                    s3[:, J, :, :].rearrange("p s c -> p (s c)"),
                                    start=(J == 0 and I % 2 == 0), stop=(J == NT - 1), skip_group_check=True)
                last.then_inc(s_l3, 1)


_INPUTS = ("adjT", "xin", "xT", "params")


def kernel(x, adj, L0_gnn_W, L1_gnn_weight, L1_gnn_bias, L2_gnn_W, L2_gnn_b, L3_gnn_weight, L3_gnn_bias):
    import concourse.bacc as bacc
    from concourse.bass_utils import run_bass_kernel_spmd

    pad = NPAD - N
    adjT = np.ascontiguousarray(np.pad(np.asarray(adj).T, ((0, pad), (0, pad))))
    xin = np.ascontiguousarray(np.pad(np.asarray(x), ((0, pad), (0, 0))).reshape(NT, P, C).transpose(1, 0, 2))
    tri = (2.0 * P * np.eye(P) - np.tril(np.ones((P, P)), -1)).astype(np.float32)
    rows = lambda b: np.broadcast_to(np.asarray(b), (P, C))
    tall = lambda w: np.pad(np.asarray(w), ((0, P - C), (0, 0)))
    twice = lambda w: np.concatenate([w, w])
    W0, W2 = np.asarray(L0_gnn_W).T, np.asarray(L2_gnn_W)
    params = np.ascontiguousarray(np.concatenate(
        [np.eye(P, dtype=np.float32), tri, tall(W0[:C]), twice(W0[C:]), tall(W2[:C]), twice(W2[C:]),
         rows(L1_gnn_bias), rows(L2_gnn_b), rows(L3_gnn_bias), tall(L1_gnn_weight), tall(L3_gnn_weight)], axis=1))
    xT = np.ascontiguousarray(np.pad(np.asarray(x), ((0, pad), (0, 0))).T)
    arrays = {"adjT": adjT, "xin": xin, "xT": xT, "params": params}

    nc = bacc.Bacc("TRN2", target_bir_lowering=False, num_devices=1)
    args = [nc.dram_tensor(n, arrays[n].shape, mybir.dt.float32, kind="ExternalInput").ap() for n in _INPUTS]
    out = nc.dram_tensor("out", (P, NT, C), mybir.dt.float32, kind="ExternalOutput").ap()
    adj_resnorm_program(nc, *args, out)
    r = run_bass_kernel_spmd(nc, [arrays], core_ids=[0])
    y = np.asarray(r.results[0]["out"])
    return np.ascontiguousarray(y.transpose(1, 0, 2).reshape(NPAD, C)[:N])
```

```python
import concourse.bass as bass
from concourse import mybir
from contextlib import ExitStack
import numpy as np

P = 128
N = 3327
NT = (N + P - 1) // P
NPAD = NT * P
C = 64
CA = C + 1
CW = 4
W = CW * P
CHUNKS = [(t, min(CW, NT - t)) for t in range(0, NT, CW)]
NC = len(CHUNKS)
NQ = NT // 2
SPLIT = 3
MAX_NEIGH = 100
LN_EPS = 1e-5
MIN_NORM = 1e-15
TANH_CLIP = 1.0 - 1e-05
LOOP_FUNCTIONS = "natural_log_exp_and_others"
LN_FLOOR = 1e-18
OFF_ID, OFF_TRI = 0, P
(OFF_W0X, OFF_W0N, OFF_W2X, OFF_W2N, OFF_B1, OFF_B2, OFF_B3, OFF_W1, OFF_W3,
 NPAR) = (2 * P + i * C for i in range(10))
KG = C + 2
BP = 96
NBP = SPLIT * SPLIT
KR = BP + NBP
DVE_Q = (3, 7, 11)
POOL_Q = tuple(q for q in range(NQ) if q not in DVE_Q)
RING = 8
MK = 5
MR = 2 * MK
WR = 5


FINISH = [(0, 4), (4, NC)]
EARLY = CHUNKS[FINISH[1][0]][0] // 2
ORDER2 = ([(c, q) for c in (0, 1) for q in range(EARLY)] + [(c, q) for c in (0, 1) for q in range(EARLY, NQ)]
          + [(c, q) for c in range(2, NC) for q in range(NQ)])
DONE2 = [ORDER2.index((c, NQ - 1)) + 1 for c in range(NC)]


def adj_resnorm_program(nc, adjT, xin, xTin, params, out):
    f32, bf16 = mybir.dt.float32, mybir.dt.bfloat16
    u8, i16 = mybir.dt.uint8, mybir.dt.int16
    ALU, ACT, AX = mybir.AluOpType, mybir.ActivationFunctionType, mybir.AxisListType.X

    PAIRS = [(A, J, min(nt, J - I0 + 1), min(nt, J - I0)) for A, (I0, nt) in enumerate(CHUNKS) for J in range(I0, NT)]
    NP_ = len(PAIRS)
    FIRST = [min(k for k, p in enumerate(PAIRS) if p[0] == A) for A in range(NC)]
    LAST = [max(k for k, p in enumerate(PAIRS) if p[0] == A) for A in range(NC)]
    MIRRORS = [sum(1 for p in PAIRS[:k + 1] if p[3]) for k in range(NP_)]
    FLUSH = [(A, max(t, I0 + 1), min(t + CW, NT)) for A, (I0, _) in enumerate(CHUNKS) for t in range(I0, NT, CW)]
    FLUSH_AT = [max(k for k, p in enumerate(PAIRS) if p[0] == A and p[1] < hi) for A, lo, hi in FLUSH]
    FLUSH_OF = {(p[0], p[1]): min(f for f in range(len(FLUSH)) if FLUSH_AT[f] >= k) for k, p in enumerate(PAIRS)}

    SIDE = [(FLUSH_AT[f] + 6, 0, f) for f in range(len(FLUSH))]
    for A in range(NC):
        turns = (6, 7, 8, 10, 11, 12, 13) if A < NC - 3 else (6, 6, 7, 7, 7, 8, 9)
        SIDE += [(LAST[A] + turn, 1 + i, A) for i, turn in enumerate(turns)]
        if A + 1 < NC:
            SIDE += [(FIRST[A] + 1 + i, 8 + i, A + 1) for i in range(3)]
    tangent_turn = {A: turn for turn, step, A in SIDE if step == 7}
    for b, (_, end) in enumerate(FINISH):
        SIDE += [(tangent_turn[end - 1] + 1 + i, 11 + i, b) for i in range(6)]
    SIDE.sort()
    LOOP = NP_ + 5

    def side_work(s, steps, between=None):
        for turn, step, c in SIDE:
            if step in steps and (turn == s or (s == LOOP - 1 and turn > s)):
                if between and turn > s:
                    between()
                steps[step](c)

    LOADS = [("c", c, q) for c in range(NC) for q in range(NQ)]
    L1_BASE = len(LOADS)
    LOADS += [("p", k, 0) for k in range(NP_)]
    L2_BASE = len(LOADS)
    LOADS += [("c", c, NQ - 1 - q) for c, q in ORDER2]

    ARRIVE, count = [], [0] * RING
    for n, (kind, k, _) in enumerate(LOADS):
        count[n % RING] += 32 if kind == "p" and PAIRS[k][3] else 16
        ARRIVE.append(count[n % RING])

    HUSE = [("m", 0)]
    for s in range(LOOP):
        if 0 <= s - 4 < NP_ and PAIRS[s - 4][3]:
            HUSE.append(("h", s - 4))
        side_work(s, {9: lambda A: HUSE.append(("m", A))})
    HB = {use: 6 + i % 2 for i, use in enumerate(HUSE)}

    ctx = ExitStack()
    with ctx:
        def sb(name, shape, dt=f32):
            return ctx.enter_context(nc.sbuf_tensor(name, shape, dt))

        def sem(name):
            return ctx.enter_context(nc.semaphore(name))

        def wait(eng, s, v):
            if v > 0:
                eng.wait_ge(s, v)

        par = sb("par", [P, NPAR])
        XA = sb("XA", [P, NT, CA])
        XB = sb("XB", [P, NT, CA])
        w8 = sb("w8", [P, NT, NPAD], u8)
        ring = sb("ring", [P, RING, 2 * W])
        gramM = sb("gramM", [P, NPAD])
        gramX = sb("gramX", [P, 2, W])
        mirror = sb("mirror", [P, NPAD])
        scratch = sb("scratch", [P, 17, W])
        pb = sb("pb", [P, 2 * CW * C + 2 * CW * KR + CW * CA])
        parts = sb("parts", [P, SPLIT, NT], bf16)
        tri = sb("tri", [P, P], bf16)
        neg = sb("neg", [P, P], bf16)
        s3 = (mirror[:, 0:NT * SPLIT * C // 2].bitcast(bf16)
              .rearrange("p (t s c) -> p t s c", s=SPLIT, c=C))
        small = sb("small", [P, 16, NT])
        cst = sb("cst", [P, 4])
        one = cst[:, 3:4]
        PS = ctx.enter_context(nc.psum_tensor("PS", [P, 8, W], f32))

        ident = par[:, OFF_ID:OFF_ID + P]
        b_all = lambda off, nt: par[:, off:off + C].unsqueeze(1).to_broadcast([P, nt, C])
        deg, dcl, rdeg0, rdeg2, x2, Bv, coef, Bc, n2, nrm, mean, var, std, rstd, sdot, Av = (
            small[:, i, :] for i in range(16))
        factor = lambda J: gramM[BP:KR, J * P:J * P + P // 2].bitcast(bf16)
        factorX = lambda A, w: gramX[BP:KR, A % 2, 0:w // 2].bitcast(bf16)
        d2b = [scratch[:, i, :] for i in (0, 1, 15)]
        rb = [scratch[:, i, :] for i in (2, 3, 4, 16)]
        tb = d2b
        lpb = [scratch[:, i, :] for i in (5, 6)]
        lmb = [scratch[:, i, :] for i in (7, 8)]
        hb = [scratch[:, i, :] for i in (9, 10)]
        kdb = [scratch[:, i, :] for i in (11, 12)]
        ktb = [scratch[:, i, :] for i in (13, 14)]
        maskb = [scratch[:, i, :].bitcast(bf16).rearrange("p (j w) -> p j w", j=2) for i in (0, 1, 2, 11, 12)]
        runb = [scratch[:, (3, 4, 5, 6, 13)[i // 2], (i % 2) * W // 2:(i % 2 + 1) * W // 2].bitcast(bf16) for i in range(MR)]
        sum_pool = [b.rearrange("p a w -> p (a w)") for b in (gramX[:, :, :], scratch[:, 15:17, :])]
        sum_dve = [scratch[:, i:i + 2, :].rearrange("p a w -> p (a w)") for i in (7, 9)]
        WB = NT * P // 2
        wide = [scratch[:, :, :].rearrange("p a w -> p (a w)")[:, i * WB:(i + 1) * WB].bitcast(i16)
                .rearrange("p (j w) -> p j w", j=NT) for i in range(WR)]
        widebf = [scratch[:, :, :].rearrange("p a w -> p (a w)")[:, i * WB:(i + 1) * WB].bitcast(bf16)
                  .rearrange("p (j w) -> p j w", j=NT) for i in range(WR)]
        accT = mirror[:, NPAD - W:NPAD]
        yb = pb[:, 0:CW * C].rearrange("p (t c) -> p t c", c=C)
        sq = pb[:, CW * C:2 * CW * C].rearrange("p (t c) -> p t c", c=C)
        rf = pb[:, 2 * CW * C:2 * CW * C + 2 * CW * KR].rearrange("p (t a c) -> p t a c", a=2, c=KR)
        pv = pb[:, 2 * CW * C + 2 * CW * KR:].rearrange("p (t c) -> p t c", c=CA)

        s_par, s_x, s_xTin, s_out = sem("s_par"), sem("s_x"), sem("s_xTin"), sem("s_out")
        s_ld = [sem(f"s_ld{i}") for i in range(RING)]
        s_cst = sem("s_cst")
        s_dve, s_act = sem("s_dve"), sem("s_act")
        s_mask, s_run, s_odd, s_w8, s_cnt, s_sumd, s_sump, s_sum, s_xT2, s_xT2c = (
            sem("s_" + n) for n in ("mask", "run", "odd", "w8", "cnt", "sumd", "sump", "sum", "xT2", "xT2c"))
        S_ = {st: {n: sem(f"{n}{st}") for n in ("grp", "accT", "z", "var", "std", "feat", "x2", "fac", "new", "xT", "xTc",
                                                 "sup")} for st in (0, 2)}
        s_d2, s_D, s_relu, s_v, s_r, s_a, s_l, s_L, s_h, s_hT, s_kd, s_kt, s_agg = (
            sem("q_" + n) for n in ("d2", "D", "relu", "v", "r", "a", "l", "L", "h", "hT", "kd", "kt", "agg"))
        s_mT, s_mc, s_rf, s_t, s_lv, s_go1, s_fl = (sem("q_" + n) for n in ("mT", "mc", "rf", "t", "lv", "go1", "fl"))
        s_pacc, s_prow, s_pagg, s_pT, s_pTc, s_pz, s_pzr, s_n2, s_nrm, s_floor, s_th, s_v1, s_sd1, s_x0, s_x1 = (
            sem("p_" + n) for n in ("acc", "row", "agg", "T", "Tc", "z", "zr", "n2", "nrm", "floor", "th", "var", "std", "x0", "x1"))
        s_wdv, s_wac, s_l3, s_y3, s_v3, s_sd3, s_o3 = (sem("t_" + n) for n in ("wdv", "wac", "l3", "y", "var", "std", "o"))

        block = ctx.enter_context(nc.Block())

        def bc(ap, nt, c=C):
            return ap.unsqueeze(2).to_broadcast([P, nt, c])

        ACC = {0: 0, 2: 4}
        slot = lambda n: ring[:, n % RING, :]

        WACT = [I for I in range(NT) if I % 3 == 2]
        WDVE = [I for I in range(NT) if I % 3 != 2]
        G3 = CHUNKS

        def summed(g):
            c, q = divmod(g, NQ)
            if q in POOL_Q:
                return s_sump, c * (len(POOL_Q) - 1) + max(POOL_Q.index(q), 1)
            return s_sumd, c * len(DVE_Q) + DVE_Q.index(q) + 1

        def tiles_of(b):
            lo, hi = FINISH[b]
            return CHUNKS[lo][0], (CHUNKS[hi][0] if hi < NC else NT)

        @block.sync
        def _(sp):
            sp.dma_start(XA[:, :, 0:C], xin).then_inc(s_x, 16)
            sp.dma_start(par[:, :], params).then_inc(s_par, 16)
            for n, (kind, k, q) in enumerate(LOADS):
                if n == RING:
                    sp.dma_start(gramM[0:C, :], xTin).then_inc(s_xTin, 16)
                m = n - RING
                if m >= 0:
                    mk, mi, mq = LOADS[m]
                    if mk == "p":
                        wait(sp, s_kd, mi + 1)
                        wait(sp, s_kt, MIRRORS[mi])
                    elif m < L1_BASE:
                        wait(sp, s_mask, m + 1)
                        wait(sp, S_[0]["grp"], m + 1)
                        wait(sp, *summed(m))
                    else:
                        wait(sp, S_[2]["grp"], m - L2_BASE + 1)
                if kind == "c":
                    I0, nt = CHUNKS[k]
                    J0 = NT - 2 - 2 * q
                    dst = slot(n).rearrange("p (j w) -> p j w", j=2)[:, :, 0:nt * P]
                    src = adjT[J0 * P:(J0 + 2) * P, I0 * P:(I0 + nt) * P].rearrange("(j p) w -> p j w", p=P)
                    sp.dma_start(dst, src).then_inc(s_ld[n % RING], 16)
                else:
                    A, J, nb, nm = PAIRS[k]
                    I0 = CHUNKS[A][0]
                    sp.dma_start(slot(n)[:, 0:nb * P],
                                 adjT[J * P:(J + 1) * P, I0 * P:(I0 + nb) * P]).then_inc(s_ld[n % RING], 16)
                    if nm:
                        dst = slot(n)[:, W:W + nm * P].rearrange("p (b f) -> p b f", f=P)
                        src = adjT[I0 * P:(I0 + nm) * P, J * P:(J + 1) * P].rearrange("(b p) f -> p b f", p=P)
                        sp.dma_start(dst, src).then_inc(s_ld[n % RING], 16)
            for g, (I0, nt) in enumerate(G3):
                wait(sp, s_o3, g + 1)
                sp.dma_start(out[:, I0:I0 + nt, :], XA[:, I0:I0 + nt, 0:C]).then_inc(s_out, 16)
            wait(sp, s_out, 16 * len(G3))

        def arrived(eng, n):
            wait(eng, s_ld[n % RING], ARRIVE[n])

        def tiles():
            for c in range(NC):
                for u in range(NT):
                    yield c * NT + u, c, u, NT - 1 - u

        @block.gpsimd
        def _(pool):
            nc.gpsimd.memset(neg[:, :], -1.0)
            nc.gpsimd.memset(cst[:, 0:1], LN_EPS)
            nc.gpsimd.memset(cst[:, 1:2], LN_FLOOR)
            nc.gpsimd.memset(cst[:, 2:3], -float(2 * P - MAX_NEIGH))
            nc.gpsimd.memset(one, 1.0).then_inc(s_cst, 1)
            for c in range(NC):
                w = CHUNKS[c][1] * P
                both = sum_pool[c % 2][:, 0:2 * w]
                load = lambda q: slot(c * NQ + q).rearrange("p (j w) -> p j w", j=2)[:, :, 0:w]
                sums = both.rearrange("p (j w) -> p j w", j=2)
                arrived(pool, c * NQ)
                wait(pool, s_sum, c - 1)
                for q in POOL_Q[1:]:
                    arrived(pool, c * NQ + q)
                    nc.gpsimd.tensor_tensor(sums, load(0) if q == 1 else sums, load(q), ALU.add).then_inc(s_sump, 1)
                    wait(pool, *summed(c * NQ + q))
            for s in range(NP_ + 3):
                k = s - 2
                if 0 <= k < NP_:
                    w = PAIRS[k][2] * P
                    wait(pool, s_l, k + 1)
                    nc.gpsimd.tensor_tensor(lpb[k % 2][:, 0:w], lpb[k % 2][:, 0:w], lmb[k % 2][:, 0:w],
                                       ALU.subtract).then_inc(s_L, 1)
                k = s - 3
                if 0 <= k < NP_:
                    w = PAIRS[k][2] * P
                    wait(pool, s_h, k + 1)
                    arrived(pool, L1_BASE + k)
                    wait(pool, s_agg, k - 1)
                    nc.gpsimd.tensor_tensor(kdb[k % 2][:, 0:w], hb[k % 2][:, 0:w], slot(L1_BASE + k)[:, 0:w],
                                       ALU.mult).then_inc(s_kd, 1)

        @block.vector
        def _(dve):
            chain = [0]

            def link(ins):
                chain[0] += 1
                ins.then_inc(s_dve, 1)
                dve.wait_ge(s_dve, chain[0])

            v = nc.vector

            def centre(y, lo, hi):
                link(v.reduce_sum(mean[:, lo:hi], y, AX))
                link(v.tensor_scalar(mean[:, lo:hi], mean[:, lo:hi], 1.0 / C, None, ALU.mult))
                return v.tensor_tensor(y, y, bc(mean[:, lo:hi], hi - lo), ALU.subtract)

            def norm_last(y, dst, lo, hi):
                link(v.reciprocal(rstd[:, lo:hi], std[:, lo:hi]))
                return v.tensor_tensor(dst, y, bc(rstd[:, lo:hi], hi - lo), ALU.mult)

            def column_sums(c):
                w = 2 * CHUNKS[c][1] * P
                wait(dve, s_sumd, (c + 1) * len(DVE_Q))
                wait(dve, s_sump, (c + 1) * (len(POOL_Q) - 1))
                v.tensor_tensor(sum_dve[c % 2][:, 0:w], sum_dve[c % 2][:, 0:w], sum_pool[c % 2][:, 0:w], ALU.add).then_inc(s_sum, 1)

            def post_b(st, c):
                I0, nt = CHUNKS[c]
                hi = I0 + nt
                q = S_[st]
                X = XA[:, I0:hi, 0:C]
                y, s = yb[:, 0:nt, :], sq[:, 0:nt, :]
                z = PS[:, 6, 0:nt * 2 * C].rearrange("p (t a c) -> p t a c", a=2, c=C)
                wait(dve, q["z"], c + 1)
                if st == 0:
                    link(v.tensor_copy(deg[:, I0:hi], PS[:, 5, 0:nt]))
                    link(v.tensor_scalar(rdeg0[:, I0:hi], deg[:, I0:hi], 1.0, None, ALU.add))
                    link(v.tensor_scalar(rdeg2[:, I0:hi], rdeg0[:, I0:hi], 1.0, None, ALU.max))
                    link(v.reciprocal(rdeg0[:, I0:hi], rdeg0[:, I0:hi]))
                    link(v.reciprocal(rdeg2[:, I0:hi], rdeg2[:, I0:hi]))
                    link(v.tensor_tensor(y, z[:, :, 0, :], bc(rdeg0[:, I0:hi], nt), ALU.mult))
                    link(v.tensor_tensor(y, z[:, :, 1, :], y, ALU.add))
                    link(v.tensor_tensor(y, y, X, ALU.add))
                else:
                    link(v.tensor_tensor(y, z[:, :, 0, :], bc(rdeg2[:, I0:hi], nt), ALU.mult))
                    link(v.tensor_tensor(y, z[:, :, 1, :], y, ALU.add))
                    link(v.tensor_tensor(y, y, b_all(OFF_B2, nt), ALU.add))
                    link(v.tensor_scalar(y, y, 0.0, None, ALU.max))
                    link(v.tensor_tensor(s, y, y, ALU.mult))
                    v.reduce_sum(n2[:, I0:hi], s, AX).then_inc(s_n2, 1)
                    wait(dve, s_nrm, len(FINISH) + c + 1)
                    link(v.tensor_scalar(nrm[:, I0:hi], nrm[:, I0:hi], 1e-12, None, ALU.max))
                    link(v.reciprocal(nrm[:, I0:hi], nrm[:, I0:hi]))
                    link(v.tensor_tensor(y, y, bc(nrm[:, I0:hi], nt), ALU.mult))
                    link(v.tensor_tensor(y, y, X, ALU.add))
                centre(y, I0, hi).then_inc(q["var"], 1)

            def post_c(st, c):
                I0, nt = CHUNKS[c]
                hi = I0 + nt
                q = S_[st]
                y, s = yb[:, 0:nt, :], sq[:, 0:nt, :]
                new = XB[:, I0:hi, 0:C]
                wait(dve, q["std"], c + 1)
                norm_last(y, new, I0, hi).then_inc(q["feat"], 1)

            def factor_parts(c):
                I0, nt = CHUNKS[c]
                hi = I0 + nt
                B, r = Bv[:, I0:hi], Av[:, I0:hi]
                wait(dve, S_[0]["x2"], c + 1)
                link(v.tensor_scalar(B, x2[:, I0:hi], -1.0, 1.0, ALU.mult, ALU.add))
                link(v.tensor_copy(parts[:, 0, I0:hi], B))
                link(v.tensor_tensor(r, B, parts[:, 0, I0:hi], ALU.subtract))
                link(v.tensor_copy(parts[:, 1, I0:hi], r))
                link(v.tensor_tensor(parts[:, 2, I0:hi], r, parts[:, 1, I0:hi], ALU.subtract))
                wait(dve, S_[0]["xT"], c)
                for i in range(SPLIT):
                    o = BP + SPLIT * i
                    last = v.tensor_copy(rf[:, 0:nt, 0, o:o + SPLIT], bc(parts[:, i, I0:hi], nt, SPLIT))
                last.then_inc(S_[0]["fac"], 1)

            def support(c):
                I0, nt = CHUNKS[c]
                wait(dve, S_[2]["sup"], c + 1)
                z = PS[:, 3, 0:nt * C].rearrange("p (t c) -> p t c", c=C)
                y, s = yb[:, 0:nt, :], sq[:, 0:nt, :]
                sc = float(2 ** (127 - MAX_NEIGH))
                link(v.tensor_scalar(y, z, sc, None, ALU.mult))
                link(v.tensor_copy(s3[:, I0:I0 + nt, 0, :], y))
                link(v.tensor_tensor(s, y, s3[:, I0:I0 + nt, 0, :], ALU.subtract))
                link(v.tensor_copy(s3[:, I0:I0 + nt, 1, :], s))
                v.tensor_tensor(s3[:, I0:I0 + nt, 2, :], s, s3[:, I0:I0 + nt, 1, :],
                                ALU.subtract).then_inc(s_x1, 1)

            link(v.memset(rf[:, :, :, :], 0.0))
            v.memset(rf[:, :, 0, C + 1:KG], 1.0)
            v.memset(rf[:, :, 1, C:C + 1], 1.0)
            v.memset(mirror[C:2 * C, 0:P], 0.0)
            wait(dve, s_par, 16)
            v.tensor_copy(tri[:, :], par[:, OFF_TRI:OFF_TRI + P]).then_inc(s_cst, 1)

            def hooks(st, c, q):
                if c < 0:
                    return
                if q == 3 and st == 0:
                    column_sums(c)
                if q == 6:
                    post_b(st, c)
                if q == 8:
                    post_c(st, c)
                if q == 10 and st == 0:
                    factor_parts(c)
                if q == 10 and st == 2:
                    support(c)

            def mask(g):
                if g >= NC * NQ:
                    return
                c, q = divmod(g, NQ)
                w = CHUNKS[c][1] * P
                arrived(dve, g)
                wait(dve, s_cnt, 2 * (g - MK) + 2)
                v.tensor_scalar(maskb[g % MK][:, :, 0:w],
                                slot(g).rearrange("p (j w) -> p j w", j=2)[:, :, 0:w],
                                0.0, None, ALU.not_equal).then_inc(s_mask, 1)

            NG = NC * NQ
            mask(0)
            for g in range(NG):
                c, q = divmod(g, NQ)
                w = CHUNKS[c][1] * P
                wait(dve, s_mask, g + 1)
                t = 2 * g
                m = maskb[g % MK]
                wait(dve, s_cnt, t + 3 - MR)
                if q > 0:
                    wait(dve, s_run, g)
                    v.tensor_tensor(runb[(t + 1) % MR][:, 0:w], runb[t % MR][:, 0:w], m[:, 1, 0:w], ALU.add).then_inc(s_odd, 1)
                mask(g + 1)
                if q > 0:
                    wait(dve, s_odd, g - c)
                    last = v.tensor_tensor(runb[(t + 2) % MR][:, 0:w], runb[(t + 1) % MR][:, 0:w], m[:, 0, 0:w], ALU.add)
                else:
                    last = v.tensor_tensor(runb[(t + 2) % MR][:, 0:w], m[:, 1, 0:w], m[:, 0, 0:w], ALU.add)
                last.then_inc(s_run, 1)
                if q in DVE_Q:
                    sums = sum_dve[c % 2][:, 0:2 * w].rearrange("p (j w) -> p j w", j=2)
                    load = slot(g).rearrange("p (j w) -> p j w", j=2)[:, :, 0:w]
                    if q == DVE_Q[0]:
                        wait(dve, S_[0]["z"], c - 1)
                        v.tensor_copy(sums, load).then_inc(s_sumd, 1)
                    else:
                        wait(dve, s_sumd, summed(g)[1] - 1)
                        v.tensor_tensor(sums, sums, load, ALU.add).then_inc(s_sumd, 1)
                hooks(0, c - 1, q)
            for q in range(NQ):
                hooks(0, NC - 1, q)

            wait(dve, S_[0]["new"], NC)
            link(v.tensor_scalar(dcl[:, :], deg[:, :], 1e-8, None, ALU.max))
            link(v.reciprocal(dcl[:, :], dcl[:, :]))
            link(v.tensor_scalar(coef[:, :], Bv[:, :], MIN_NORM, 0.5, ALU.max, ALU.mult))
            link(v.tensor_tensor(coef[:, :], coef[:, :], dcl[:, :], ALU.mult))
            v.tensor_tensor(Bc[:, :], Bv[:, :], coef[:, :], ALU.mult).then_inc(s_go1, 1)

            def gram_rows(A):
                I0, nt = CHUNKS[A]
                hi = I0 + nt
                wait(dve, s_mT, A)
                v.tensor_copy(rf[:, 0:nt, 1, 0:C], XB[:, I0:hi, 0:C])
                v.tensor_copy(rf[:, 0:nt, 1, C + 1:KG], x2[:, I0:hi].unsqueeze(2))
                rows = rf[:, 0:nt, 1, BP:KR].rearrange("p t (a b) -> p t a b", b=SPLIT)
                for i in range(SPLIT):
                    last = v.tensor_copy(rows[:, :, :, i], bc(parts[:, i, I0:hi], nt, SPLIT))
                last.then_inc(s_rf, 1)

            def flush(f):
                A, lo, hi = FLUSH[f]
                if lo >= hi:
                    return
                wait(dve, s_agg, FLUSH_AT[f] + 1)
                wait(dve, s_fl, f)
                src = PS[C:2 * C, 2 + f % 2, (lo % CW) * P:(lo % CW + hi - lo) * P]
                dst = mirror[C:2 * C, lo * P:hi * P]
                if A == 0:
                    v.tensor_copy(dst, src).then_inc(s_fl, 1)
                else:
                    v.tensor_tensor(dst, src, dst, ALU.add).then_inc(s_fl, 1)

            def aggregate(A):
                lo, nt = CHUNKS[A]
                hi = lo + nt
                X = XB[:, lo:hi, 0:C]
                rows = PS[:, A % 2, 0:nt * P].rearrange("p (t a c) -> p t a c", a=2, c=C)
                V, U = pv[:, 0:nt, 0:C], pv[:, 0:nt, C:CA]
                p1, p2 = yb[:, 0:nt, :], sq[:, 0:nt, :]
                wait(dve, s_prow, A + 1)
                wait(dve, s_pz, A)
                link(v.tensor_copy(pv[:, 0:nt, 1:CA], rows[:, :, 0, :]))
                link(v.tensor_tensor(pv[:, 0:nt, 1:CA], rows[:, :, 1, :], pv[:, 0:nt, 1:CA], ALU.add))
                link(v.tensor_reduce(pv[:, 0:nt, 0:1], pv[:, 0:nt, 1:C], AX, ALU.add, negate=True))
                link(v.tensor_tensor(p1, V, X, ALU.mult))
                link(v.reduce_sum(sdot[:, lo:hi], p1, AX))
                link(v.scalar_tensor_tensor(Av[:, lo:hi].unsqueeze(2), sdot[:, lo:hi].unsqueeze(2), -2.0, U, ALU.mult, ALU.add))
                link(v.tensor_tensor(Av[:, lo:hi], Av[:, lo:hi], coef[:, lo:hi], ALU.mult))
                link(v.tensor_tensor(p1, X, bc(Av[:, lo:hi], nt), ALU.mult))
                link(v.tensor_tensor(p2, V, bc(Bc[:, lo:hi], nt), ALU.mult))
                v.tensor_tensor(p2, p2, p1, ALU.subtract).then_inc(s_pagg, 1)

            def tangent(A):
                lo, nt = CHUNKS[A]
                hi = lo + nt
                z = PS[:, A % 2, 0:nt * C].rearrange("p (t c) -> p t c", c=C)
                wait(dve, s_pz, A + 1)
                link(v.tensor_tensor(XA[:, lo:hi, 0:C], z, b_all(OFF_B1, nt), ALU.add))
                link(v.tensor_tensor(yb[:, 0:nt, :], XA[:, lo:hi, 0:C], XA[:, lo:hi, 0:C], ALU.mult))
                v.reduce_sum(n2[:, lo:hi], yb[:, 0:nt, :], AX).then_inc(s_pzr, 1)

            def inverse_norm(b):
                lo, hi = tiles_of(b)
                wait(dve, s_nrm, b + 1)
                v.tensor_scalar(nrm[:, lo:hi], nrm[:, lo:hi], MIN_NORM, None, ALU.max).then_inc(s_floor, 1)
                wait(dve, s_floor, b + 1)
                link(v.reciprocal(Av[:, lo:hi], nrm[:, lo:hi]))

            def exp_map(b):
                lo, hi = tiles_of(b)
                Y = XA[:, lo:hi, 0:C]
                wait(dve, s_th, b + 1)
                link(v.tensor_tensor(Av[:, lo:hi], Av[:, lo:hi], sdot[:, lo:hi], ALU.mult))
                link(v.tensor_tensor(Y, Y, bc(Av[:, lo:hi], hi - lo), ALU.mult))
                link(v.tensor_tensor(Y, Y, XB[:, lo:hi, 0:C], ALU.add))
                link(centre(Y, lo, hi))
                for I0, nt in CHUNKS[slice(*FINISH[b])]:
                    link(v.tensor_tensor(yb[:, 0:nt, :], XA[:, I0:I0 + nt, 0:C], XA[:, I0:I0 + nt, 0:C], ALU.mult))
                    last = v.reduce_sum(var[:, I0:I0 + nt], yb[:, 0:nt, :], AX)
                    if I0 + nt < hi:
                        link(last)
                last.then_inc(s_v1, 1)

            def normalise(b):
                lo, hi = tiles_of(b)
                wait(dve, s_sd1, b + 1)
                v.tensor_tensor(XA[:, lo:hi, 0:C], XA[:, lo:hi, 0:C], bc(rstd[:, lo:hi], hi - lo),
                                ALU.mult).then_inc(s_x0 if b == 0 else s_x1, 1)

            steps = {0: flush, 3: aggregate, 7: tangent, 8: gram_rows, 12: inverse_norm, 14: exp_map, 16: normalise}
            gram_rows(0)
            for s in range(-1, LOOP):
                k = s - 1
                if 0 <= k < NP_:
                    w = PAIRS[k][2] * P
                    wait(dve, s_r, k + 1)
                    v.tensor_tensor(tb[k % 3][:, 0:w], d2b[k % 3][:, 0:w], rb[k % 4][:, 0:w], ALU.mult).then_inc(s_t, 1)
                    wait(dve, s_t, k + 1)
                    v.tensor_scalar(tb[k % 3][:, 0:w], tb[k % 3][:, 0:w], TANH_CLIP, None, ALU.min).then_inc(s_a, 1)
                k = s - 3
                if 0 <= k < NP_:
                    w = PAIRS[k][2] * P
                    wait(dve, s_L, k + 1)
                    wait(dve, s_kd, k - 1)
                    wait(dve, s_hT, MIRRORS[k - 2] if k >= 2 else 0)
                    v.tensor_tensor(hb[k % 2][:, 0:w], lpb[k % 2][:, 0:w], rb[k % 4][:, 0:w], ALU.mult).then_inc(s_h, 1)
                k = s + 1
                if k < NP_:
                    w = PAIRS[k][2] * P
                    wait(dve, s_D, k + 1)
                    wait(dve, s_relu, k + 1)
                    wait(dve, s_h, k - 3)
                    v.scalar_tensor_tensor(rb[k % 4][:, 0:w], PS[:, 4 + k % 2, 0:w], MIN_NORM, d2b[k % 3][:, 0:w],
                                           ALU.max, ALU.mult).then_inc(s_v, 1)
                k = s - 4
                if 0 <= k < NP_ and PAIRS[k][3]:
                    wm = PAIRS[k][3] * P
                    wait(dve, s_hT, MIRRORS[k])
                    arrived(dve, L1_BASE + k)
                    wait(dve, s_agg, k - 1)
                    v.tensor_tensor(ktb[k % 2][:, 0:wm], PS[:, HB[("h", k)], 0:wm],
                                    slot(L1_BASE + k)[:, W:W + wm], ALU.mult).then_inc(s_kt, 1)
                side_work(s, steps)
            def widen(I):
                wait(dve, s_l3, I - WR + 1)
                v.tensor_scalar(wide[I % WR], w8[:, :, I * P:(I + 1) * P], float(P), None,
                                ALU.mult).then_inc(s_wdv, 1)

            for I in WDVE:
                if I < WR:
                    widen(I)
            for c in range(NC):
                for q in range(NQ):
                    hooks(2, c, q)
            todo = [I for I in WDVE if I >= WR]
            for g, (I0, nt) in enumerate(G3):
                hi = I0 + nt
                while todo and todo[0] < hi + WR:
                    widen(todo.pop(0))
                y, s = yb[:, 0:nt, :], sq[:, 0:nt, :]
                wait(dve, s_o3, g)
                wait(dve, s_l3, hi)
                for i in range(I0, hi, 2):
                    part = PS[:, (i // 2) % 4, 0:2 * SPLIT * C].rearrange("p (t s c) -> p t c s", s=SPLIT, c=C)
                    last = v.tensor_reduce(y[:, i - I0:i - I0 + 2, :], part, AX, ALU.add)
                last.then_inc(s_y3, 1)
                wait(dve, s_y3, g + 1)
                link(v.tensor_tensor(y, y, XB[:, I0:hi, 0:C], ALU.add))
                link(v.tensor_tensor(y, y, b_all(OFF_B3, nt), ALU.add))
                centre(y, I0, hi).then_inc(s_v3, 1)
                wait(dve, s_sd3, g + 1)
                norm_last(y, XA[:, I0:hi, 0:C], I0, hi).then_inc(s_o3, 1)

        @block.scalar
        def _(act):
            a = nc.scalar

            def copy_accT(st, c):
                nt = CHUNKS[c][1]
                wait(act, S_[st]["grp"], (c + 1) * NQ if st == 0 else DONE2[c])
                wait(act, S_[st]["z"], c)
                a.copy(accT[:, 0:nt * P], PS[:, ACC[st] + c % 2, 0:nt * P]).then_inc(S_[st]["accT"], 1)

            def deviation(lo, hi, ready, n, done):
                wait(act, ready, n)
                a.activation(std[:, lo:hi], var[:, lo:hi], ACT.Sqrt, bias=cst[:, 0:1], scale=1.0 / C).then_inc(done, 1)

            act_chain = [0]

            def link(ins):
                act_chain[0] += 1
                ins.then_inc(s_act, 1)
                act.wait_ge(s_act, act_chain[0])

            def squares(y, dst, lo, hi, done=None):
                for i in range(hi - lo):
                    last = a.activation(sq[:, i, :], y[:, i, :], ACT.Square, accum_out=dst[:, lo + i:lo + i + 1])
                if done is None:
                    link(last)
                else:
                    last.then_inc(done, 1)

            def norm_std(st, c):
                I0, nt = CHUNKS[c]
                if st == 2:
                    wait(act, s_n2, c + 1)
                    a.activation(nrm[:, I0:I0 + nt], n2[:, I0:I0 + nt], ACT.Sqrt).then_inc(s_nrm, 1)
                wait(act, S_[st]["var"], c + 1)
                squares(yb, var, I0, I0 + nt)
                deviation(I0, I0 + nt, S_[st]["var"], c + 1, S_[st]["std"])

            def features(c):
                I0, nt = CHUNKS[c]
                hi = I0 + nt
                wait(act, S_[0]["feat"], c + 1)
                squares(XB[:, I0:hi, 0:C], x2, I0, hi, S_[0]["x2"])
                wait(act, S_[0]["x2"], c + 1)
                wait(act, S_[0]["xT"], c)
                a.activation(XB[:, I0:hi, C:CA], x2[:, I0:hi].unsqueeze(2), ACT.Identity, bias=1.0)
                a.copy(rf[:, 0:nt, 0, C:C + 1], x2[:, I0:hi].unsqueeze(2))
                a.mul(rf[:, 0:nt, 0, 0:C], XB[:, I0:hi, 0:C], -2.0).then_inc(S_[0]["new"], 1)

            def copy_xT(st, c):
                I0, nt = CHUNKS[c]
                wait(act, S_[st]["xT"], c + 1)
                rows = KG if st == 0 else C
                if st == 0:
                    for i in range(nt):
                        a.copy(factor(I0 + i), PS[BP:KR, 7, i * P:(i + 1) * P])
                a.copy(gramM[0:rows, I0 * P:(I0 + nt) * P], PS[0:rows, 7, 0:nt * P]).then_inc(S_[st]["xTc"], 1)

            def hooks(st, c, u):
                if c < 0:
                    return
                if u == 3:
                    copy_accT(st, c)
                if u == 15:
                    norm_std(st, c)
                if u == 18 and st == 0:
                    features(c)
                if u == 22:
                    copy_xT(st, c)

            wait(act, s_cst, 2)
            for t, c, u, J in tiles():
                I0, nt = CHUNKS[c]
                wait(act, s_cnt, t + 1)
                a.activation(w8[:, J, I0 * P:(I0 + nt) * P], PS[:, 2 + t % 3, 0:nt * P], ACT.Relu,
                             bias=cst[:, 2:3]).then_inc(s_w8, 1)
                hooks(0, c - 1, u)
            for u in range(NT):
                hooks(0, NC - 1, u)

            def moving_copy(A):
                nt = CHUNKS[A][1]
                wait(act, s_mT, A + 1)
                wait(act, s_D, FIRST[A - 1] if A >= 2 else 0)
                bank = HB[("m", A)]
                a.copy(gramX[0:KG, A % 2, 0:nt * P], PS[0:KG, bank, 0:nt * P])
                a.copy(factorX(A, nt * P), PS[BP:KR, bank, 0:nt * P]).then_inc(s_mc, 1)

            def acc_copy(A):
                lo, nt = CHUNKS[A]
                wait(act, s_agg, LAST[A] + 1)
                a.copy(mirror[0:C, lo * P:(lo + nt) * P], PS[0:C, A % 2, 0:nt * P]).then_inc(s_pacc, 1)

            def agg_copy(A):
                lo, nt = CHUNKS[A]
                wait(act, s_pT, A + 1)
                a.copy(mirror[0:C, lo * P:(lo + nt) * P], PS[0:C, A % 2, 0:nt * P]).then_inc(s_pTc, 1)

            def norms(b):
                lo, hi = tiles_of(b)
                wait(act, s_pzr, FINISH[b][1])
                a.activation(nrm[:, lo:hi], n2[:, lo:hi], ACT.Sqrt).then_inc(s_nrm, 1)
                a.preload_act_table_set(LOOP_FUNCTIONS)

            def tanhs(b):
                lo, hi = tiles_of(b)
                wait(act, s_floor, b + 1)
                a.activation(sdot[:, lo:hi], nrm[:, lo:hi], ACT.Tanh).then_inc(s_th, 1)
                a.preload_act_table_set(LOOP_FUNCTIONS)

            def deviations(b):
                lo, hi = tiles_of(b)
                wait(act, s_v1, b + 1)
                link(a.activation(std[:, lo:hi], var[:, lo:hi], ACT.Ln, bias=cst[:, 0:1], scale=1.0 / C))
                a.activation(rstd[:, lo:hi], std[:, lo:hi], ACT.Exp, scale=-0.5).then_inc(s_sd1, 1)

            steps = {1: acc_copy, 5: agg_copy, 10: moving_copy, 11: norms, 13: tanhs, 15: deviations}
            a.preload_act_table_set(LOOP_FUNCTIONS)
            moving_copy(0)
            for s in range(-1, LOOP):
                k = s - 2
                if 0 <= k < NP_:
                    w = PAIRS[k][2] * P
                    wait(act, s_a, k + 1)
                    wait(act, s_h, k - 1)
                    a.activation(lpb[k % 2][:, 0:w], tb[k % 3][:, 0:w], ACT.Ln, bias=1.0)
                    a.activation(lmb[k % 2][:, 0:w], tb[k % 3][:, 0:w], ACT.Ln, bias=1.0, scale=-1.0).then_inc(s_l, 1)
                k = s + 1
                if k < NP_:
                    w = PAIRS[k][2] * P
                    wait(act, s_d2, k + 1)
                    wait(act, s_l, k - 2)
                    a.activation(d2b[k % 3][:, 0:w], PS[:, 4 + k % 2, 0:w], ACT.Relu).then_inc(s_relu, 1)
                k = s
                if 0 <= k < NP_:
                    w = PAIRS[k][2] * P
                    wait(act, s_v, k + 1)
                    a.activation(rb[k % 4][:, 0:w], rb[k % 4][:, 0:w], ACT.Ln, bias=cst[:, 1:2]).then_inc(s_lv, 1)
                    wait(act, s_lv, k + 1)
                    a.activation(rb[k % 4][:, 0:w], rb[k % 4][:, 0:w], ACT.Exp, scale=-0.5).then_inc(s_r, 1)
                side_work(s, steps)
            def widen(I):
                wait(act, s_l3, I - WR + 1)
                a.activation(wide[I % WR], w8[:, :, I * P:(I + 1) * P], ACT.Copy, scale=float(P)).then_inc(s_wac, 1)

            wait(act, s_x1, 1)
            for I in WACT:
                if I < WR:
                    widen(I)
            for c in range(NC):
                I0, nt = CHUNKS[c]
                wait(act, s_xT2, c + 1)
                a.copy(gramM[0:C, I0 * P:(I0 + nt) * P], PS[0:C, 7, 0:nt * P]).then_inc(s_xT2c, 1)
            for c in range(NC):
                for u in range(NT):
                    hooks(2, c, u)
            todo = [I for I in WACT if I >= WR]
            for g, (I0, nt) in enumerate(G3):
                while todo and todo[0] < I0 + nt + WR:
                    widen(todo.pop(0))
                wait(act, s_v3, g + 1)
                squares(yb, var, I0, I0 + nt)
                deviation(I0, I0 + nt, s_v3, g + 1, s_sd3)

        @block.tensor
        def _(pe):
            T = nc.tensor

            def project(st, c):
                I0, nt = CHUNKS[c]
                WX, WN = (OFF_W0X, OFF_W0N) if st == 0 else (OFF_W2X, OFF_W2N)
                wait(pe, s_xTin, 16)
                wait(pe, S_[st]["accT"], c + 1)
                wait(pe, S_[st]["var"], c)
                for i in range(nt):
                    o = i * 2 * C
                    cols = slice((I0 + i) * P, (I0 + i + 1) * P)
                    T.matmul(PS[:, 6, o:o + C], accT[:, i * P:(i + 1) * P], par[:, WN:WN + C],
                             start=True, stop=(st == 0))
                    if st == 2:
                        T.matmul(PS[:, 6, o:o + C], gramM[0:C, cols], par[0:C, WN:WN + C], start=False, stop=True)
                    last = T.matmul(PS[:, 6, o + C:o + 2 * C], gramM[0:C, cols], par[0:C, WX:WX + C],
                                    start=True, stop=True)
                if st == 0:
                    wait(pe, s_sum, c + 1)
                    w = nt * P
                    for i in range(nt):
                        T.matmul(PS[:, 5, i:i + 1], sum_dve[c % 2][:, i * P:(i + 1) * P], one, start=True, stop=False)
                        last = T.matmul(PS[:, 5, i:i + 1], sum_dve[c % 2][:, w + i * P:w + (i + 1) * P], one,
                                        start=False, stop=True)
                last.then_inc(S_[st]["z"], 1)

            def x_transposes(st, c):
                I0, nt = CHUNKS[c]
                wait(pe, S_[st]["new" if st == 0 else "feat"], c + 1)
                if st == 0:
                    wait(pe, S_[0]["fac"], c + 1)
                wait(pe, S_[st]["xTc"], c)
                for i in range(nt):
                    src = rf[:, i, 0, :] if st == 0 else XB[:, I0 + i, 0:C]
                    rows = KR if st == 0 else C
                    last = T.transpose(PS[0:rows, 7, i * P:(i + 1) * P], src, ident)
                last.then_inc(S_[st]["xT"], 1)

            def supports(c):
                I0, nt = CHUNKS[c]
                wait(pe, S_[2]["xTc"], c + 1)
                wait(pe, s_x1, 1 + c)
                for i in range(nt):
                    t = I0 + i
                    last = T.matmul(PS[:, 3, i * C:(i + 1) * C], gramM[0:C, t * P:(t + 1) * P],
                                    par[0:C, OFF_W3:OFF_W3 + C], start=True, stop=True)
                last.then_inc(S_[2]["sup"], 1)

            def hooks(st, c, q):
                if c < 0:
                    return
                if q == 4:
                    project(st, c)
                if q == 10:
                    x_transposes(st, c)
                if q == 11 and st == 2:
                    supports(c)

            def products(st, n, c, first, last, tiles):
                w = CHUNKS[c][1] * P
                arrived(pe, n)
                if first:
                    wait(pe, S_[st]["accT"], c - 1)
                for half, (J, jj) in enumerate(tiles):
                    ins = T.matmul(PS[half * C:(half + 1) * C, ACC[st] + c % 2, 0:w], XA[:, J, 0:C],
                                   slot(n)[:, jj * W:jj * W + w], start=first, stop=last, skip_group_check=True)
                ins.then_inc(S_[st]["grp"], 1)

            def stage0():
                for g in range(NC * NQ):
                    c, q = divmod(g, NQ)
                    w = CHUNKS[c][1] * P
                    J0 = NT - 2 - 2 * q
                    products(0, g, c, q == 0, q == NQ - 1, ((J0 + 1, 1), (J0, 0)))
                    for u in (2 * q, 2 * q + 1):
                        t, jj = c * NT + u, 1 - u % 2
                        bank = PS[:, 2 + t % 3, 0:w]
                        wait(pe, s_mask, g + 1)
                        wait(pe, s_w8, t - 2)
                        last = T.matmul(bank, tri[:, :], maskb[g % MK][:, jj, 0:w], start=True, stop=(u == 0))
                        if u == 1:
                            last = T.matmul(bank, neg[:, :], maskb[g % MK][:, 1, 0:w], start=False, stop=True)
                        elif u > 1:
                            wait(pe, s_run, g if u % 2 == 0 else g + 1)
                            last = T.matmul(bank, neg[:, :], runb[t % MR][:, 0:w], start=False, stop=True)
                        last.then_inc(s_cnt, 1)
                    hooks(0, c - 1, q)
                for q in range(NQ):
                    hooks(0, NC - 1, q)

            group2 = [0]

            def stage2(upto):
                for g in range(group2[0], upto):
                    c, q = ORDER2[g]
                    if g == 0:
                        wait(pe, s_v, NP_)
                        wait(pe, s_x0, 1)
                    if g == 2 * EARLY:
                        wait(pe, s_x1, 1)
                    products(2, L2_BASE + g, c, q == 0, q == NQ - 1, ((2 * q, 0), (2 * q + 1, 1)))
                    if 0 <= g - 2 * EARLY < NC:
                        own_transposes(g - 2 * EARLY)
                    if g >= 2 * NQ:
                        hooks(2, c - 1, q)
                    hooks(2, 0, {1: 4, 7: 10, 8: 11}.get(g - DONE2[0]))
                group2[0] = upto

            def own_transposes(c):
                I0, nt = CHUNKS[c]
                wait(pe, s_xT2c, c)
                for i in range(nt):
                    last = T.transpose(PS[0:C, 7, i * P:(i + 1) * P], XA[:, I0 + i, 0:C], ident)
                last.then_inc(s_xT2, 1)

            wait(pe, s_par, 16)
            wait(pe, s_x, 16)
            wait(pe, s_cst, 2)
            stage0()

            def moving_transposes(A):
                nt = CHUNKS[A][1]
                wait(pe, s_rf, A + 1)
                release(("m", A))
                for i in range(nt):
                    last = T.transpose(PS[0:KR, HB[("m", A)], i * P:(i + 1) * P], rf[:, i, 1, :], ident)
                last.then_inc(s_mT, 1)

            def release(use):
                n = HUSE.index(use)
                if n >= 2:
                    kind, i = HUSE[n - 2]
                    if kind == "m":
                        wait(pe, s_mc, i + 1)
                    else:
                        wait(pe, s_kt, MIRRORS[i])

            def distances(k):
                A, J, nb, _ = PAIRS[k]
                w = nb * P
                wait(pe, s_mc, A + 1)
                wait(pe, s_v, k - 1)
                T.matmul(PS[:, 4 + k % 2, 0:w], gramM[0:KG, J * P:(J + 1) * P], gramX[0:KG, A % 2, 0:w],
                         start=True, stop=False, skip_group_check=True).then_inc(s_d2, 1)

            def denominators(k):
                A, J, nb, _ = PAIRS[k]
                w = nb * P
                wait(pe, s_relu, k + 1)
                T.matmul(PS[:, 4 + k % 2, 0:w], factor(J), factorX(A, w), start=False, stop=True,
                         skip_group_check=True).then_inc(s_D, 1)

            def sum_rows(A):
                lo, nt = CHUNKS[A]
                wait(pe, s_pacc, A + 1)
                wait(pe, s_fl, max(f for f in range(len(FLUSH)) if FLUSH[f][0] <= A and FLUSH[f][1] < lo + nt) + 1)
                for i in range(nt):
                    last = T.transpose(PS[:, A % 2, i * P:(i + 1) * P], mirror[:, (lo + i) * P:(lo + i + 1) * P], ident)
                last.then_inc(s_prow, 1)

            def agg_transposes(A):
                wait(pe, s_pagg, A + 1)
                for i in range(CHUNKS[A][1]):
                    last = T.transpose(PS[0:C, A % 2, i * P:(i + 1) * P], sq[:, i, :], ident)
                last.then_inc(s_pT, 1)

            def agg_project(A):
                lo, nt = CHUNKS[A]
                wait(pe, s_pTc, A + 1)
                for i in range(nt):
                    last = T.matmul(PS[:, A % 2, i * C:(i + 1) * C], mirror[0:C, (lo + i) * P:(lo + i + 1) * P],
                                    par[0:C, OFF_W1:OFF_W1 + C], start=True, stop=True)
                last.then_inc(s_pz, 1)

            steps = {2: sum_rows, 4: agg_transposes, 6: agg_project, 9: moving_transposes}
            wait(pe, S_[0]["xTc"], NC)
            wait(pe, s_w8, NC * NT)
            wait(pe, s_go1, 1)
            moving_transposes(0)
            distances(0)
            for s in range(-1, LOOP):
                if s + 2 < NP_:
                    distances(s + 2)
                if s + 1 < NP_:
                    denominators(s + 1)
                k = s - 4
                if 0 <= k < NP_:
                    wait(pe, s_h, k + 1)
                    if PAIRS[k][3]:
                        release(("h", k))
                        for i in range(PAIRS[k][3]):
                            last = T.transpose(PS[:, HB[("h", k)], i * P:(i + 1) * P], hb[k % 2][:, i * P:(i + 1) * P], ident)
                        last.then_inc(s_hT, 1)
                k = s - 5
                if 0 <= k < NP_:
                    A, J, nb, nm = PAIRS[k]
                    I0 = CHUNKS[A][0]
                    f = FLUSH_OF[(A, J)]
                    if k == FIRST[A]:
                        wait(pe, s_pzr, A - 1)
                    wait(pe, s_kd, k + 1)
                    if nm:
                        wait(pe, s_kt, MIRRORS[k])
                        wait(pe, s_fl, f - 1)
                    for i in range(nb):
                        last = T.matmul(PS[0:C, A % 2, i * P:(i + 1) * P], XB[:, J, 1:CA], kdb[k % 2][:, i * P:(i + 1) * P],
                                        start=(k == FIRST[A] and i == 0), stop=(J == NT - 1), skip_group_check=True)
                        if i < nm:
                            last = T.matmul(PS[C:2 * C, 2 + f % 2, (J % CW) * P:(J % CW + 1) * P], XB[:, I0 + i, 1:CA],
                                            ktb[k % 2][:, i * P:(i + 1) * P], start=(J == FLUSH[f][1] and i == 0),
                                            stop=(i == nm - 1), skip_group_check=True)
                    last.then_inc(s_agg, 1)
                side_work(s, steps, lambda: stage2(min(group2[0] + 1, 2 * EARLY)))

            stage2(NC * NQ)

            def decayed(targets, lo, hi):
                for I in targets:
                    if lo == 0:
                        if I in WACT:
                            wait(pe, s_wac, WACT.index(I) + 1)
                        else:
                            wait(pe, s_wdv, WDVE.index(I) + 1)
                        if I % CW == 0:
                            wait(pe, s_y3, I // CW - 1)
                    for J in range(lo, hi):
                        o = (I % 2) * SPLIT * C
                        last = T.matmul(PS[:, (I // 2) % 4, o:o + SPLIT * C], widebf[I % WR][:, J, :],
                                        s3[:, J, :, :].rearrange("p s c -> p (s c)"),
                                        start=(J == 0 and I % 2 == 0), stop=(J == NT - 1), skip_group_check=True)
                    if hi == NT:
                        last.then_inc(s_l3, 1)

            J5, J6 = CHUNKS[-2][0], CHUNKS[-1][0]
            project(2, NC - 1)
            wait(pe, s_x1, NC - 1)
            decayed((0, 1), 0, J5)
            x_transposes(2, NC - 1)
            decayed((2,), 0, J5)
            supports(NC - 1)
            decayed((3,), 0, J5)
            wait(pe, s_x1, NC)
            decayed(range(4), J5, J6)
            wait(pe, s_x1, 1 + NC)
            decayed(range(4), J6, NT)
            for I in range(4, NT):
                decayed((I,), 0, NT)


_INPUTS = ("adjT", "xin", "xT", "params")


def kernel(x, adj, L0_gnn_W, L1_gnn_weight, L1_gnn_bias, L2_gnn_W, L2_gnn_b, L3_gnn_weight, L3_gnn_bias):
    import concourse.bacc as bacc
    from concourse.bass_utils import run_bass_kernel_spmd

    pad = NPAD - N
    adjT = np.ascontiguousarray(np.pad(np.asarray(adj).T, ((0, pad), (0, pad))))
    xin = np.ascontiguousarray(np.pad(np.asarray(x), ((0, pad), (0, 0))).reshape(NT, P, C).transpose(1, 0, 2))
    tri = (2.0 * P * np.eye(P) - np.tril(np.ones((P, P)), -1)).astype(np.float32)
    rows = lambda b: np.broadcast_to(np.asarray(b), (P, C))
    tall = lambda w: np.pad(np.asarray(w), ((0, P - C), (0, 0)))
    twice = lambda w: np.concatenate([w, w])
    W0, W2 = np.asarray(L0_gnn_W).T, np.asarray(L2_gnn_W)
    params = np.ascontiguousarray(np.concatenate(
        [np.eye(P, dtype=np.float32), tri, tall(W0[:C]), twice(W0[C:]), tall(W2[:C]), twice(W2[C:]),
         rows(L1_gnn_bias), rows(L2_gnn_b), rows(L3_gnn_bias), tall(L1_gnn_weight), tall(L3_gnn_weight)], axis=1))
    xT = np.ascontiguousarray(np.pad(np.asarray(x), ((0, pad), (0, 0))).T)
    arrays = {"adjT": adjT, "xin": xin, "xT": xT, "params": params}

    nc = bacc.Bacc("TRN2", target_bir_lowering=False, num_devices=1)
    args = [nc.dram_tensor(n, arrays[n].shape, mybir.dt.float32, kind="ExternalInput").ap() for n in _INPUTS]
    out = nc.dram_tensor("out", (P, NT, C), mybir.dt.float32, kind="ExternalOutput").ap()
    adj_resnorm_program(nc, *args, out)
    r = run_bass_kernel_spmd(nc, [arrays], core_ids=[0])
    y = np.asarray(r.results[0]["out"])
    return np.ascontiguousarray(y.transpose(1, 0, 2).reshape(NPAD, C)[:N])
```
